# Optimizing a Trainium2 kernel written in Bass

```python
import numpy as np
import jax
import jax.numpy as jnp

def _softmax(x, axis=-1):
    return jax.nn.softmax(x, axis=axis)

def _gelu(x):
    return jax.nn.gelu(x, approximate=True)

def _silu(x):
    return jax.nn.silu(x)

def _sigmoid(x):
    return jax.nn.sigmoid(x)

def _layernorm(x, axis=-1, eps=1e-05):
    m = jnp.mean(x, axis=axis, keepdims=True)
    v = jnp.var(x, axis=axis, keepdims=True)
    return (x - m) / jnp.sqrt(v + eps)

def _scatter_add(tgt, idx, src, axis=0):
    return tgt.at[idx].add(src)

def _segment_sum(src, seg, n):
    return jax.ops.segment_sum(src, seg, n)
kernel_name = 'mk_flamingo_gated_d1_seqx_r8_caec54'

def setup_inputs(seed: int=0):
    np.random.seed(seed)
    _w = jnp.asarray

    def _rec_inputs():
        import jax
        import jax.numpy as jnp
        _rk = jax.random.key(seed)
        x = 7.22e-05 + 1 * jax.random.normal(jax.random.fold_in(_rk, 1), (4, 256, 256), jnp.float32)
        _lenS = 256 - jax.random.randint(jax.random.fold_in(_rk, 7), (4,), 0, max(1, 256 // 4) + 1, jnp.int32)
        _lenS2 = 256 - jax.random.randint(jax.random.fold_in(_rk, 8), (4,), 0, max(1, 256 // 4) + 1, jnp.int32)
        _ctx_1024P = jax.random.normal(jax.random.fold_in(_rk, 11), (4, 16, 128), jnp.float32)
        _ctx_1024c = jax.random.dirichlet(jax.random.fold_in(_rk, 511), 0.3 * jnp.ones((16,), jnp.float32), (4, 256))
        _ctx_1024t = jnp.einsum('bsk,bkd->bsd', _ctx_1024c, _ctx_1024P)
        _ctx_1024t = _ctx_1024t * jax.lax.rsqrt(jnp.mean(jnp.square(_ctx_1024t)) + 1e-12) * 0.953939
        ctx_1024 = -1.39393e-06 + 0.999914 * (_ctx_1024t + 0.3 * jax.random.normal(jax.random.fold_in(_rk, 611), (4, 256, 128), jnp.float32))
        fside_BxSx2_0 = jax.random.uniform(jax.random.fold_in(_rk, 12), (4, 256, 2), jnp.float32, 0.0, 0.999707)
        _g = jax.random.normal(jax.random.fold_in(_rk, 9001), (2, 1), jnp.float32)
        _g = jnp.sign(_g) * jnp.maximum(jnp.abs(_g), 1.0) + (_g == 0) * 1.0
        g_xattn = _g[0]
        g_ffn = _g[1]
        return (x, ctx_1024, fside_BxSx2_0, g_xattn, g_ffn)
    x, ctx_1024, fside_BxSx2_0, g_xattn, g_ffn = _rec_inputs()

    def _L0_xattn_setup():
        import jax, jax.numpy as jnp
        import numpy as np
        DIM = 256
        CTX_DIM = 128
        N_HEADS = 32
        HEAD_DIM = DIM // N_HEADS
        POS_DIM = 2
        B, N, CTXN = (2, 256, 256)
        ROPE_BASE = 10000.0

        def apply_axial_rope(x, pos):
            b, n, h, d = x.shape
            p = pos.shape[-1]
            dpa = d // p
            half = dpa // 2
            freqs = ROPE_BASE ** (-jnp.arange(half, dtype=x.dtype) / half)
            ang = pos[..., :, None] * freqs
            cos = jnp.cos(ang)[:, :, None, :, :]
            sin = jnp.sin(ang)[:, :, None, :, :]
            xr = x.reshape(b, n, h, p, half, 2)
            x1, x2 = (xr[..., 0], xr[..., 1])
            out = jnp.stack([x1 * cos - x2 * sin, x1 * sin + x2 * cos], axis=-1)
            return out.reshape(b, n, h, d)
        key = jax.random.key(seed)
        ks = jax.random.split(key, 8)
        x = jax.random.normal(ks[0], (B, N, DIM), jnp.float32)
        ctx = jax.random.normal(ks[1], (B, CTXN, CTX_DIM), jnp.float32)
        pos_map = jax.random.uniform(ks[2], (B, N, POS_DIM), jnp.float32)
        ctx_pos_map = jax.random.uniform(ks[3], (B, CTXN, POS_DIM), jnp.float32)
        Wq = jax.random.normal(ks[4], (DIM, DIM), jnp.float32) / np.sqrt(DIM)
        Wkv = jax.random.normal(ks[5], (CTX_DIM, 2 * DIM), jnp.float32) / np.sqrt(CTX_DIM)
        Wout = jax.random.normal(ks[6], (DIM, DIM), jnp.float32) / np.sqrt(DIM)
        bout = jnp.zeros((DIM,), jnp.float32)
        return {'x': x, 'ctx': ctx, 'pos_map': pos_map, 'ctx_pos_map': ctx_pos_map, 'Wq': Wq, 'Wkv': Wkv, 'Wout': Wout, 'bout': bout}
    _L0_xattn_all = _L0_xattn_setup()
    _L0_xattn_in = {k: v for k, v in _L0_xattn_all.items() if k in ('Wq', 'Wkv', 'Wout', 'bout')}
    del _L0_xattn_all

    def _L0_ffn_setup():
        import jax, jax.numpy as jnp
        import numpy as np
        TOP_K = 8
        CAPACITY = 128
        key = jax.random.key(seed)
        k1, k2, k3, k4 = jax.random.split(key, 4)
        B, S, H, E, I = (2, 128, 256, 64, 96)
        hidden_states = jax.random.normal(k1, (B, S, H), dtype=jnp.float32)
        router_weight = jax.random.normal(k2, (E, H), dtype=jnp.float32) * 0.02
        gate_up_proj = jax.random.normal(k3, (E, H, 2 * I), dtype=jnp.float32) * 0.02
        down_proj = jax.random.normal(k4, (E, I, H), dtype=jnp.float32) * 0.02
        return {'hidden_states': hidden_states, 'router_weight': router_weight, 'gate_up_proj': gate_up_proj, 'down_proj': down_proj}
    _L0_ffn_all = _L0_ffn_setup()
    _L0_ffn_in = {k: v for k, v in _L0_ffn_all.items() if k in ('router_weight', 'gate_up_proj', 'down_proj')}
    del _L0_ffn_all
    return {'x': x, 'ctx_1024': ctx_1024, 'fside_BxSx2_0': fside_BxSx2_0, 'g_xattn': g_xattn, 'g_ffn': g_ffn, 'L0_xattn_Wq': _L0_xattn_in['Wq'], 'L0_xattn_Wkv': _L0_xattn_in['Wkv'], 'L0_xattn_Wout': _L0_xattn_in['Wout'], 'L0_xattn_bout': _L0_xattn_in['bout'], 'L0_ffn_router_weight': _L0_ffn_in['router_weight'], 'L0_ffn_gate_up_proj': _L0_ffn_in['gate_up_proj'], 'L0_ffn_down_proj': _L0_ffn_in['down_proj']}

def reference(x, ctx_1024, fside_BxSx2_0, g_xattn, g_ffn, L0_xattn_Wq, L0_xattn_Wkv, L0_xattn_Wout, L0_xattn_bout, L0_ffn_router_weight, L0_ffn_gate_up_proj, L0_ffn_down_proj):
    import jax
    import jax.numpy as jnp

    def _L0_xattn_ref(x, ctx, pos_map, ctx_pos_map, Wq, Wkv, Wout, bout):
        import jax, jax.numpy as jnp
        import numpy as np
        DIM = 256
        CTX_DIM = 128
        N_HEADS = 32
        HEAD_DIM = DIM // N_HEADS
        POS_DIM = 2
        B, N, CTXN = (2, 256, 256)
        ROPE_BASE = 10000.0

        def apply_axial_rope(x, pos):
            b, n, h, d = x.shape
            p = pos.shape[-1]
            dpa = d // p
            half = dpa // 2
            freqs = ROPE_BASE ** (-jnp.arange(half, dtype=x.dtype) / half)
            ang = pos[..., :, None] * freqs
            cos = jnp.cos(ang)[:, :, None, :, :]
            sin = jnp.sin(ang)[:, :, None, :, :]
            xr = x.reshape(b, n, h, p, half, 2)
            x1, x2 = (xr[..., 0], xr[..., 1])
            out = jnp.stack([x1 * cos - x2 * sin, x1 * sin + x2 * cos], axis=-1)
            return out.reshape(b, n, h, d)
        b, n, _ = x.shape
        ctx_n = ctx.shape[1]
        q = (x @ Wq).reshape(b, n, N_HEADS, HEAD_DIM)
        k, v = jnp.split(ctx @ Wkv, 2, axis=-1)
        k = k.reshape(b, ctx_n, N_HEADS, HEAD_DIM)
        v = v.reshape(b, ctx_n, N_HEADS, HEAD_DIM)
        q = apply_axial_rope(q, pos_map)
        k = apply_axial_rope(k, ctx_pos_map)
        scale = 1.0 / np.sqrt(HEAD_DIM).astype(np.float32)
        logits = jnp.einsum('bqhd,bkhd->bhqk', q, k) * scale
        w = jax.nn.softmax(logits, axis=-1)
        attn = jnp.einsum('bhqk,bkhd->bqhd', w, v)
        attn = attn.reshape(b, n, N_HEADS * HEAD_DIM)
        return attn @ Wout + bout

    def _L0_ffn_ref(hidden_states, router_weight, gate_up_proj, down_proj):
        import jax, jax.numpy as jnp
        import numpy as np
        TOP_K = 8
        CAPACITY = 128
        B, S, H = hidden_states.shape
        E = router_weight.shape[0]
        K, C = (TOP_K, CAPACITY)
        x = hidden_states.reshape(-1, H)
        logits = x @ router_weight.T
        probs = jax.nn.softmax(logits, axis=-1)
        topw, topi = jax.lax.top_k(probs, K)
        topw = topw / jnp.sum(topw, axis=-1, keepdims=True)
        flat_e = topi.reshape(-1)
        oh = jax.nn.one_hot(flat_e, E, dtype=jnp.int32)
        pos = jnp.take_along_axis(jnp.cumsum(oh, axis=0), flat_e[:, None], axis=1)[:, 0] - 1
        x_rep = jnp.repeat(x, K, axis=0)
        xe = jnp.zeros((E, C, H), x.dtype).at[flat_e, pos].set(x_rep, mode='drop')
        gu = jnp.einsum('ech,ehf->ecf', xe, gate_up_proj)
        g, u = jnp.split(gu, 2, axis=-1)
        h = jax.nn.silu(g) * u
        ye = jnp.einsum('eci,eih->ech', h, down_proj)
        valid = pos < C
        y_flat = jnp.where(valid[:, None], ye[flat_e, jnp.minimum(pos, C - 1)], 0.0)
        y = jnp.sum(y_flat.reshape(-1, K, H) * topw.reshape(-1, K)[..., None], axis=1)
        return y.reshape(B, S, H)
    x = x + jnp.tanh(g_xattn[0]) * _L0_xattn_ref(_layernorm(x, axis=-1), ctx_1024, fside_BxSx2_0, fside_BxSx2_0, L0_xattn_Wq, L0_xattn_Wkv, L0_xattn_Wout, L0_xattn_bout)
    x = x + jnp.tanh(g_ffn[0]) * _L0_ffn_ref(_layernorm(x, axis=-1), L0_ffn_router_weight, L0_ffn_gate_up_proj, L0_ffn_down_proj)
    return x

_drawn_inputs = setup_inputs


def setup_inputs(seed=0):
    import zlib

    import numpy as np

    out = dict(_drawn_inputs(seed))
    spreads = {'L0_xattn_bout': (0.0, 0.1)}
    factors = {'L0_ffn_router_weight': 8.0, 'L0_ffn_gate_up_proj': 8.0, 'L0_ffn_down_proj': 8.0}
    for name, (base, spread) in spreads.items():
        noise = np.random.default_rng([zlib.crc32(name.encode()), seed]).standard_normal(out[name].shape)
        drawn = base * np.exp(spread * noise) if base else spread * noise
        out[name] = jnp.asarray(drawn.astype(out[name].dtype))
    for name, factor in factors.items():
        out[name] = (out[name] * factor).astype(out[name].dtype)
    return out
```

```python
from contextlib import ExitStack

import concourse.bass as bass
from concourse import mybir

P = 128
F32 = mybir.dt.float32
BF16 = mybir.dt.bfloat16
U32 = mybir.dt.uint32
I32 = mybir.dt.int32
ALU = mybir.AluOpType
ACT = mybir.ActivationFunctionType
AX = mybir.AxisListType

PARTS = 64
PROD = 48
MAXROWS = 50
VCOLS = 32
DEN = 8
ACCS = 4
RING = 8
TOPK = 8
TWO_PI = 6.283185307179586
PI_F = 3.1415925
MAGIC = 12582912.0


def need(eng, sem, value):
    if isinstance(value, int) and value <= 0:
        return
    eng.wait_ge(sem, value)


def hold(eng, sem, value):
    eng.wait_ge(sem, value)
    eng.nop(nofuse=True)


class Links:

    def __init__(self, eng, sem, base):
        self.eng, self.sem, self.base, self.n = eng, sem, base, 0

    def link(self, ins):
        self.n += 1
        ins.then_inc(self.sem, 1)
        hold(self.eng, self.sem, self.base + self.n)


def two_part(v):
    hi = float(int(v * 256)) / 256
    return hi, v - hi


def flamingo(nc, x, ctx_1024, fside_BxSx2_0, g_xattn, g_ffn, L0_xattn_Wq, L0_xattn_Wkv, L0_xattn_Wout,
             L0_xattn_bout, L0_ffn_router_weight, L0_ffn_gate_up_proj, L0_ffn_down_proj, out):
    B, N, D = x.shape
    CD = ctx_1024.shape[2]
    HD = 8
    H = D // HD
    T = B * N
    NT = T // P
    TB = N // P
    G = H // 4
    E, _, I2 = L0_ffn_gate_up_proj.shape
    I = I2 // 2
    C = P
    DC = D // P
    ROW = D + E + 4
    ID = D + E
    ITEMS = B * G
    SCALE = float(HD) ** -0.5
    NSC = TB * TOPK
    HALF = HD // 4
    LATE = E // 4
    assert (N, D, CD, H, E, I, TB, G, DC, HALF) == (256, 256, 128, 32, 64, 96, 2, 8, 2, 2)

    xf = x.rearrange("b n d -> (b n) d").rearrange("(t p) d -> p t d", p=P)
    of = out.rearrange("b n d -> (b n) d").rearrange("(t p) d -> p t d", p=P)
    ctxf = ctx_1024.rearrange("b n d -> (b n) d").rearrange("(t p) d -> p t d", p=P)
    posf = fside_BxSx2_0.rearrange("b n d -> (b n) d").rearrange("(t p) d -> p t d", p=P)
    wgu_src = L0_ffn_gate_up_proj.rearrange("e (p c) f -> p e (c f)", c=DC)
    wd_src = L0_ffn_down_proj.rearrange("e i h -> i e h")

    slots = nc.dram_tensor("slots", [E * C, ROW], F32, kind="Internal").ap()
    acc = [nc.dram_tensor(f"acc{a}", [T + P, D], F32, kind="Internal").ap() for a in range(ACCS)]

    with ExitStack() as ctx:
        arena = (nc.sbuf_base + 63) // 64 * 64
        top = [arena]

        def at(name, shape, dt, offset):
            return nc.alloc_sbuf_tensor_at(name, shape, dt, offset=offset)

        def sb(name, shape, dt):
            n = 4 if dt != BF16 else 2
            for s in shape[1:]:
                n *= s
            here = top[0]
            top[0] = (here + n + 31) // 32 * 32
            return at(name, shape, dt, here)

        def sem(name):
            return ctx.enter_context(nc.semaphore(name))

        def psum(name, shape, dt):
            return ctx.enter_context(nc.psum_tensor(name, shape, dt))

        wd = sb("wd", [P, E, D], F32)
        gu_base = top[0]
        wgu = sb("wgu", [P, E, DC * I2], F32)
        late = gu_base + LATE * DC * I2 * 4
        end_of_weights = top[0]
        top[0] = late
        qsp = sb("qsp", [P, 2 * TB * H * PARTS], BF16)
        ksp = sb("ksp", [P, 2 * TB * H * PARTS], BF16)
        probs = sb("probs", [P, 2, 4 * 2 * N], F32)
        vaug = sb("vaug", [P, TB, H * VCOLS], F32)
        qk = sb("qk", [P, 2, 4 * N], BF16)
        qm = sb("qm", [P, 2 * N], BF16)
        vstage = sb("vstage", [P, TB, D], F32)
        qsb = sb("qsb", [P, TB * D], F32)
        ksb = sb("ksb", [P, TB * D], F32)
        rt = sb("rt", [P, TB * D], F32)
        rt2 = sb("rt2", [P, TB * D], F32)
        assert top[0] <= end_of_weights
        top[0] = end_of_weights
        xall = sb("xall", [P, NT, D], F32)
        identf = sb("identf", [P, P], F32)
        identb = sb("identb", [P, P], BF16)
        before = sb("before", [P, P], BF16)
        onesb = sb("onesb", [P, P], BF16)
        onesr = sb("onesr", [1, P], F32)
        slot0 = sb("slot0", [P, TB * E], F32)
        slot_i = sb("slot_i", [P, TB * E], I32)
        ids = sb("ids", [P, NT], I32)
        half_neg = sb("half_neg", [P, NT], F32)
        gates = sb("gates", [P, 4], F32)
        wrT = sb("wrT", [P, DC, E], F32)
        stat2 = sb("stat2", [P, TB, 6], F32)
        mv2 = sb("mv2", [P, TB, 2], F32)
        rstd2 = sb("rstd2", [P, TB], F32)
        ybuf = sb("ybuf", [P, TB, D], F32)
        wbuf = sb("wbuf", [P, TB, E], F32)
        rows = sb("rows", [P, TB, ROW], F32)
        idx = sb("idx", [P, TB, TOPK], U32)
        logit = sb("logit", [P, TB, E], F32)
        best = sb("best", [P, TB, 8], F32)
        nbest = sb("nbest", [P, TB], F32)
        cut = sb("cut", [P, TB, E], F32)
        chosen = sb("chosen", [P, TB, E], F32)
        chosenb = sb("chosenb", [P, TB, E], BF16)
        seen = sb("seen", [P, E], BF16)
        expl = sb("expl", [P, TB, E], F32)
        wsum = sb("wsum", [P, TB], F32)
        wrec = sb("wrec", [P, TB], F32)
        place = sb("place", [P, TB, E], F32)
        drop = sb("drop", [P, TB, E], F32)
        best8 = sb("best8", [P, TB, TOPK], F32)
        shared = top[0]
        rest = sb("rest", [P, TB * D], F32)
        xn = sb("xn", [P, TB, D], F32)
        ctxc = sb("ctxc", [P, TB, CD], F32)
        ctxT = sb("ctxT", [P, N], F32)
        wq = sb("wq", [P, DC * D], F32)
        wkv = sb("wkv", [P, 2 * D], F32)
        otsb = sb("otsb", [P, 2, N], F32)
        attn = sb("attn", [P, TB, D], F32)
        attnT = sb("attnT", [P, DC, N], F32)
        xT = sb("xT", [P, DC, N], F32)
        wout = sb("wout", [P, DC * D], F32)
        bout = sb("bout", [1, D], F32)
        pos = sb("pos", [P, NT, 2], F32)
        cosT = sb("cosT", [P, NT, HD], F32)
        sinT = sb("sinT", [P, NT, HD], F32)
        nmax = sb("nmax", [P, 2, TB, 4], F32)
        rden = sb("rden", [P, TB, 4], F32)
        stat1 = sb("stat1", [P, NT, 6], F32)
        mv1 = sb("mv1", [P, NT, 2], F32)
        rstd1 = sb("rstd1", [P, NT], F32)
        end_attn = top[0]
        assert end_attn <= nc.sbuf_usable_end, (end_attn, nc.sbuf_usable_end)
        top[0] = shared
        xe = sb("xe", [P, RING, ROW], F32)
        ye = sb("ye", [P, RING, D], F32)
        xeT = sb("xeT", [P, 2, DC * C], F32)
        hsb = sb("hsb", [P, 2, I], F32)
        sg = sb("sg", [P, 2, I], F32)
        hT = sb("hT", [P, 2, C], F32)
        assert top[0] <= nc.sbuf_usable_end
        fin = [at(f"fin{a}", [P, NT, D], F32, arena + a * NT * D * 4) for a in range(ACCS)]
        ctxall = at("ctxall", [P, NT, CD], F32, late - 4 * NT * CD)
        rw = at("rw", [E, D], F32, late - 4 * NT * CD - 4 * D)
        ang_at = late - 4 * NT * CD - 4 * D - 6 * NT * 4 * 4
        ang, turns, red, cosr, over = (at(f"angle{i}", [P, NT, 4], F32, ang_at + i * NT * 4 * 4) for i in range(5))
        zrow = at("zrow", [P, ROW], F32, (ang_at - 4 * ROW) // 32 * 32)
        early = LATE - 8

        psT1 = psum("psT1", [P, 4 * N], BF16)
        psT2 = psum("psT2", [P, 4 * N], BF16)
        psS = [psum(f"psS{i}", [P, 2 * N], F32) for i in range(2)]
        psST = [psum(f"psST{i}", [P, 2 * N], F32) for i in range(2)]
        psO = psum("psO", [P, 2 * N], F32)
        psX = psum("psX", [P, 2 * N], F32)
        bank_xT = [psS[0], psS[1]]
        bank_gu = [psST[0], psST[1]]
        bank_hT = [psO, psX]
        bank_y = [psT1[:, :].bitcast(F32), psT2[:, :].bitcast(F32)]

        x_in, ctx_in, small_in, wproj_in = sem("x_in"), sem("ctx_in"), sem("small_in"), sem("wproj_in")
        wd_in = [sem(f"wd_in{i}") for i in range(4)]
        wgu_in = [sem(f"wgu_in{i}") for i in range(E // 8)]
        acc_done = [sem(f"acc_done{a}") for a in range(ACCS)]
        slots_filled, acc_filled = sem("slots_filled"), sem("acc_filled")
        consts, zrow_ready = sem("consts"), sem("zrow_ready")
        table_links, sin_done, tables = sem("table_links"), sem("sin_done"), sem("tables")
        rw_T, wrT_ready = sem("rw_T"), sem("wrT_ready")
        stats1, rstd1_ready, gates_ready = sem("stats1"), sem("rstd1_ready"), sem("gates_ready")
        stat_links = sem("stat_links")
        xn_ready, ctxc_ready = sem("xn_ready"), sem("ctxc_ready")
        psx_full, psx_free = sem("psx_full"), sem("psx_free")
        v_staged = sem("v_staged")
        q_rot, k_rot, rope_links = sem("q_rot"), sem("k_rot"), sem("rope_links")
        split_links, split_done = sem("split_links"), sem("split_done")
        pads = sem("pads")
        t1_full, qk_ready = sem("t1_full"), sem("qk_ready")
        s_full, max_done, mhi_done, m_ready = sem("s_full"), sem("max_done"), sem("mhi_done"), sem("m_ready")
        t2_full, qm_ready = sem("t2_full"), sem("qm_ready")
        st_full, exp_done, pv_done = sem("st_full"), sem("exp_done"), sem("pv_done")
        ot_ready, rden_done, v_ready = sem("ot_ready"), sem("rden_done"), sem("v_ready")
        x1_ready, stats2, rstd2_ready, y_ready = sem("x1_ready"), sem("stats2"), sem("rstd2_ready"), sem("y_ready")
        ln_links, route_links = sem("ln_links"), sem("route_links")
        nbest_ready, expl_ready, chosen_ready, w_ready, idx_ready = (
            sem("nbest_ready"), sem("expl_ready"), sem("chosen_ready"), sem("w_ready"), sem("idx_ready"))
        rows_ready = sem("rows_ready")
        scattered = sem("scattered")
        xe_in = [sem(f"xe_in{i}") for i in range(RING)]
        xeT_full, xeT_ready, gu_full, sg_ready, h_ready = (
            sem("xeT_full"), sem("xeT_ready"), sem("gu_full"), sem("sg_ready"), sem("h_ready"))
        hT_full, hT_ready, y_full, ye_ready = sem("hT_full"), sem("hT_ready"), sem("y_full"), sem("ye_ready")
        fin_in = [sem(f"fin_in{a}") for a in range(ACCS)]
        pool_links = sem("pool_links")
        fin_links, out_ready, out_done = sem("fin_links"), sem("out_ready"), sem("out_done")

        prep = ["ctxT", "xnT", "q", "kv0", "kv1"]
        SLOT = {0: (None, "ctxT"), 1: ("xnT", None), 2: ("q", "kv0"), 3: ("attnT", "kv1"), 4: ("wout", None),
                5: (None, "ynT"), 6: (None, "logit"), 7: (None, "rank")}
        epi = ["attnT", "wout", "ynT", "logit", "rank"]

        def jobs_of(has_prep, has_epi, first):
            found = []
            for g in range(G):
                for name in SLOT[g]:
                    if name and (has_prep if name in prep else has_epi):
                        found.append(name)
                if not (first and g < 3):
                    found.append(f"ot{g}")
            return found

        FIRST, MIDDLE, LAST = jobs_of(True, False, True), jobs_of(True, True, False), jobs_of(False, True, False)
        TAIL = ["ot0", "ot1", "ot2", *epi]
        BASE1 = len(prep) + len(FIRST)
        BASE_LAST = BASE1 + (B - 2) * len(MIDDLE)
        BASE_TAIL = BASE_LAST + len(LAST)

        def use(region, b, name):
            if region == "pro":
                return prep.index(name)
            if region == "first":
                return len(prep) + FIRST.index(name)
            if region == "middle":
                return BASE1 + (b - 1) * len(MIDDLE) + MIDDLE.index(name)
            if region == "last":
                return BASE_LAST + LAST.index(name)
            return BASE_TAIL + TAIL.index(name)

        def jobs_at(region, g):
            has = {"first": prep, "middle": prep + epi, "last": epi, "tail": []}[region]
            return [n if n in has else None for n in SLOT[g]]

        def item(region, b, g, back):
            if region == "tail" and g >= back:
                return None
            if g >= back:
                return b, g - back
            return None if region == "first" else (b - 1, g - back + G)

        def regions(eng, body):
            body("first", 0)
            with eng.Fori(1, B - 1) as b:
                body("middle", b)
            body("last", B - 1)

        block = ctx.enter_context(nc.Block())

        @block.sync
        def _(sp):
            sp.dma_start(xall[:], xf).then_inc(x_in, 16)
            sp.dma_start(pos[:], posf).then_inc(small_in, 16)
            sp.dma_start(wq[:], L0_xattn_Wq.rearrange("(p c) n -> p (c n)", c=DC)).then_inc(wproj_in, 16)
            sp.dma_start(ctxall[:], ctxf).then_inc(ctx_in, 16)
            sp.dma_start(wkv[:], L0_xattn_Wkv).then_inc(wproj_in, 16)
            sp.dma_start(rw[:], L0_ffn_router_weight).then_inc(small_in, 16)
            sp.dma_start(gates[:, 0:1], g_xattn.partition_broadcast(P)).then_inc(small_in, 16)
            sp.dma_start(gates[:, 1:2], g_ffn.partition_broadcast(P)).then_inc(small_in, 16)
            sp.dma_start(wout[:], L0_xattn_Wout.rearrange("(p c) n -> p (c n)", c=DC)).then_inc(wproj_in, 16)
            sp.dma_start(bout[:], L0_xattn_bout.rearrange("(a n) -> a n", a=1)).then_inc(wproj_in, 16)
            sp.wait_ge(zrow_ready, 1)
            sp.dma_start(slots.rearrange("(e c) r -> c e r", c=C),
                         zrow[:].unsqueeze(1).to_broadcast([P, E, ROW])).then_inc(slots_filled, 16)
            for i in range(4):
                n = E // 4
                sp.dma_start(wd[0:I, i * n:(i + 1) * n, :], wd_src[:, i * n:(i + 1) * n, :]).then_inc(wd_in[i], 16)
            for a in range(ACCS):
                sp.dma_start(acc[a].rearrange("(t p) d -> p t d", p=P),
                             zrow[:, 0:D].unsqueeze(1).to_broadcast([P, NT + 1, D])).then_inc(acc_filled, 16)

            def load_gu(i):
                sp.dma_start(wgu[:, 8 * i:8 * i + 8, :], wgu_src[:, 8 * i:8 * i + 8, :]).then_inc(wgu_in[i], 16)

            for i in range(early // 8):
                load_gu(i)
            sp.wait_ge(ctxc_ready, B)
            sp.wait_ge(wrT_ready, 1)
            sp.wait_ge(tables, 1)
            sp.wait_ge(slots_filled, 16)
            sp.wait_ge(acc_filled, 16 * ACCS)
            load_gu(early // 8)
            sp.wait_ge(pv_done, ITEMS)
            sp.wait_ge(qm_ready, ITEMS)
            for i in range(early // 8 + 1, E // 8):
                load_gu(i)
            sp.wait_ge(scattered, 16 * NSC * B)

            def load_slots(e, r):
                sp.dma_start(xe[:, r, :], slots[bass.ds(e * C, C), :]).then_inc(xe_in[r], 16)

            for r in range(RING):
                load_slots(r, r)
            with sp.Fori(1, E // RING) as it:
                for r in range(RING):
                    sp.wait_ge(acc_done[r % ACCS], 16 * (2 * it + r // ACCS - 1))
                    load_slots(it * RING + r, r)
            for a in range(ACCS):
                sp.wait_ge(acc_done[a], 16 * (E // ACCS))
                for h in range(2):
                    sp.dma_start(fin[a][:, h * 4:h * 4 + 4, :],
                                 acc[a].rearrange("(t p) d -> p t d", p=P)[:, h * 4:h * 4 + 4, :]).then_inc(fin_in[a], 16)
            for h in range(2):
                sp.wait_ge(out_ready, h + 1)
                sp.dma_start(of[:, h * 4:h * 4 + 4, :], xall[:, h * 4:h * 4 + 4, :]).then_inc(out_done, 16)
            sp.wait_ge(out_done, 32)

        @block.tensor
        def _(pe):
            pe.wait_ge(consts, 1)
            pe.wait_ge(small_in, 64)

            def bank_x(region, b, name):
                need(pe, psx_free, use(region, b, name))

            for c in range(DC):
                last = pe.transpose(psO[:, c * E:(c + 1) * E], rw[:, c::DC], identf[0:E, 0:E])
            last.then_inc(rw_T, 1)

            def do(region, b, name):
                bank_x(region, b, name)
                if name == "xnT":
                    pe.wait_ge(xn_ready, b + 2)
                    for t in range(TB):
                        for c in range(DC):
                            last = pe.transpose(psX[:, (c * TB + t) * P:(c * TB + t + 1) * P], xn[:, t, c::DC], identf[:])
                elif name == "ctxT":
                    pe.wait_ge(ctxc_ready, b + 2)
                    for t in range(TB):
                        last = pe.transpose(psX[:, t * P:(t + 1) * P], ctxc[:, t, :], identf[:])
                elif name == "q":
                    for t in range(TB):
                        for c in range(DC):
                            last = pe.matmul(psX[:, t * D:(t + 1) * D], xT[:, c, t * P:(t + 1) * P],
                                             wq[:, c * D:(c + 1) * D], start=(c == 0), stop=(c == DC - 1))
                elif name in ("kv0", "kv1"):
                    t = int(name[2])
                    last = pe.matmul(psX[:, 0:2 * D], ctxT[:, t * P:(t + 1) * P], wkv[:], start=True, stop=True)
                elif name == "attnT":
                    for t in range(TB):
                        for c in range(DC):
                            last = pe.transpose(psX[:, (c * TB + t) * P:(c * TB + t + 1) * P], attn[:, t, c::DC], identf[:])
                elif name == "wout":
                    for t in range(TB):
                        pe.matmul(psX[:, t * D:(t + 1) * D], onesr[:], bout[:], start=True, stop=False)
                        for c in range(DC):
                            last = pe.matmul(psX[:, t * D:(t + 1) * D], attnT[:, c, t * P:(t + 1) * P],
                                             wout[:, c * D:(c + 1) * D], start=False, stop=(c == DC - 1))
                elif name == "ynT":
                    pe.wait_ge(y_ready, b)
                    for t in range(TB):
                        for c in range(DC):
                            last = pe.transpose(psX[:, (c * TB + t) * P:(c * TB + t + 1) * P], ybuf[:, t, c::DC], identf[:])
                elif name == "logit":
                    for t in range(TB):
                        for c in range(DC):
                            last = pe.matmul(psX[:, t * E:(t + 1) * E], xT[:, c, t * P:(t + 1) * P], wrT[:, c, :],
                                             start=(c == 0), stop=(c == DC - 1))
                elif name == "rank":
                    pe.wait_ge(chosen_ready, b)
                    pe.matmul(psX[:, 0:E], before[:], chosenb[:, 0, :], start=True, stop=False)
                    pe.matmul(psX[:, 0:E], onesb[:], seen[:], start=False, stop=True)
                    pe.matmul(psX[:, E:2 * E], before[:], chosenb[:, 1, :], start=True, stop=False)
                    pe.matmul(psX[:, E:2 * E], onesb[:], chosenb[:, 0, :], start=False, stop=False)
                    last = pe.matmul(psX[:, E:2 * E], onesb[:], seen[:], start=False, stop=True)
                last.then_inc(psx_full, 1)

            def t1(b, g, par):
                if g == 0:
                    pe.wait_ge(split_done, 2 * (b + 1))
                need(pe, qk_ready, b * G + g)
                for src, o in ((qsp, 0), (ksp, 2 * N)):
                    for ct in range(2):
                        for t in range(TB):
                            col = par * (TB * H * PARTS) + t * H * PARTS + (4 * g + 2 * ct) * PARTS
                            last = pe.transpose(psT1[:, o + ct * N + t * P:o + ct * N + (t + 1) * P],
                                                src[:, bass.ds(col, P)], identb[:])
                last.then_inc(t1_full, 1)

            def logits(b, g, j):
                a, ct = 64 * (j % 2), j // 2
                need(pe, max_done, b * H + 4 * g + j - 1)
                for t in range(TB):
                    last = pe.matmul(psS[j % 2][:, t * N:(t + 1) * N],
                                     qk[a:a + PROD, g % 2, ct * N + t * P:ct * N + (t + 1) * P],
                                     qk[a:a + PROD, g % 2, 2 * N + ct * N:2 * N + (ct + 1) * N], start=True, stop=True)
                last.then_inc(s_full, 1)

            def t2(b, g, par):
                hold(pe, m_ready, b * G + g + 1)
                for ct in range(2):
                    for t in range(TB):
                        col = par * (TB * H * PARTS) + t * H * PARTS + (4 * g + 2 * ct) * PARTS
                        last = pe.transpose(psT2[:, ct * N + t * P:ct * N + (t + 1) * P],
                                            qsp[:, bass.ds(col, P)], identb[:])
                last.then_inc(t2_full, 1)

            def shifted(b, g, j):
                a, ct = 64 * (j % 2), j // 2
                if j == 0:
                    pe.wait_ge(qm_ready, b * G + g + 1)
                need(pe, exp_done, b * H + 4 * g + j - 1)
                for kc in range(TB):
                    last = pe.matmul(psST[j % 2][:, kc * N:(kc + 1) * N],
                                     qk[a:a + MAXROWS, g % 2, 2 * N + ct * N + kc * P:2 * N + ct * N + (kc + 1) * P],
                                     qm[a:a + MAXROWS, ct * N:(ct + 1) * N], start=True, stop=True)
                last.then_inc(st_full, 1)

            def pv(b, g):
                pe.wait_ge(exp_done, b * H + 4 * g + 4)
                need(pe, ot_ready, b * G + g)
                if g == 0:
                    pe.wait_ge(v_ready, b + 1)
                for kc in range(TB):
                    for j in range(4):
                        last = pe.matmul(psO[32 * j:32 * j + 32, 0:N],
                                         vaug[:, kc, (4 * g + j) * VCOLS:(4 * g + j + 1) * VCOLS],
                                         probs[:, g % 2, (2 * j + kc) * N:(2 * j + kc + 1) * N],
                                         start=(kc == 0), stop=(kc == TB - 1))
                last.then_inc(pv_done, 1)

            def ot(region, b, g, bi, gi):
                bank_x(region, b, f"ot{g}")
                pe.wait_ge(ot_ready, bi * G + gi + 1)
                for t in range(TB):
                    last = pe.transpose(psX[:, t * P:(t + 1) * P], otsb[:, gi % 2, t * P:(t + 1) * P], identf[:])
                last.then_inc(psx_full, 1)

            def step(region, b, g):
                one, two, three = (item(region, b, g, back) for back in (1, 2, 3))
                new = region != "tail"
                jobs = jobs_at(region, g)
                if new:
                    pe.wait_ge(qk_ready, b * G + g + 1)
                    logits(b, g, 0)
                    logits(b, g, 1)
                if one:
                    t2(*one, one[0] % 2)
                if jobs[0]:
                    do(region, b, jobs[0])
                if one:
                    shifted(*one, 0)
                if new:
                    logits(b, g, 2)
                if one:
                    shifted(*one, 1)
                if new:
                    logits(b, g, 3)
                if one:
                    shifted(*one, 2)
                    shifted(*one, 3)
                if jobs[1]:
                    do(region, b, jobs[1])
                if two:
                    pv(*two)
                if new and g < G - 1:
                    t1(b, g + 1, b % 2)
                elif new and region != "last":
                    t1(b + 1, 0, (b + 1) % 2)
                if three:
                    ot(region, b, g, *three)

            pe.wait_ge(wproj_in, 64)
            pe.wait_ge(wrT_ready, 1)
            for name in prep:
                do("pro", -1, name)
            pe.wait_ge(pads, 3)
            t1(0, 0, 0)

            def batch(region, b):
                for g in range(G):
                    step(region, b, g)

            regions(pe, batch)
            for g in range(3):
                step("tail", B, g)
            for name in epi:
                do("tail", B, name)

            pe.wait_ge(psx_free, BASE_TAIL + len(TAIL))
            for s in (*wd_in, *wgu_in):
                pe.wait_ge(s, 16)

            def to_cols(e, par, r, rounds):
                pe.wait_ge(xe_in[r], 16 * rounds)
                need(pe, xeT_ready, e - 1)
                for c in range(DC):
                    last = pe.transpose(bank_xT[par][:, c * C:(c + 1) * C], xe[:, r, c:D:DC], identf[:])
                last.then_inc(xeT_full, 1)

            def gate_up(e, par):
                pe.wait_ge(xeT_ready, e + 1)
                need(pe, h_ready, e - 1)
                for c in range(DC):
                    last = pe.matmul(bank_gu[par][:, 0:I2], xeT[:, par, c * C:(c + 1) * C],
                                     wgu[:, e, c * I2:(c + 1) * I2], start=(c == 0), stop=(c == DC - 1))
                last.then_inc(gu_full, 1)

            def turn_h(e, par):
                pe.wait_ge(h_ready, e + 1)
                need(pe, hT_ready, e - 1)
                pe.transpose(bank_hT[par][0:I, 0:C], hsb[:, par, :], identf[:]).then_inc(hT_full, 1)

            def down(e, par):
                pe.wait_ge(hT_ready, e + 1)
                need(pe, ye_ready, e - 1)
                pe.matmul(bank_y[par][:, 0:D], hT[0:I, par, :], wd[0:I, e, :], start=True, stop=True).then_inc(y_full, 1)

            def estep(s, k, it=0):
                first, final = isinstance(s, int) and s < 1, isinstance(s, int) and s > E - 3
                if not final:
                    e = s + 2
                    to_cols(e, k % 2, (k + 2) % RING, it + (k + 2) // RING + 1)
                if not (isinstance(s, int) and (s + 1 < 0 or s + 1 >= E)):
                    gate_up(s + 1, (k + 1) % 2)
                if not (isinstance(s, int) and (s < 0 or s >= E)):
                    turn_h(s, k % 2)
                if not first:
                    down(s - 1, (k + 1) % 2)

            LOOPS = (E - 5) // RING
            for s in range(-2, 3):
                estep(s, s)
            with pe.Fori(0, LOOPS) as it:
                for k in range(3, RING + 3):
                    estep(it * RING + k, k, it)
            for s in range(LOOPS * RING + 3, E + 1):
                estep(s, s)

        @block.scalar
        def _(act):
            act.wait_ge(small_in, 64)
            act.wait_ge(tables, 1)
            c2 = cosT[:].rearrange("p t (f a) -> p t f a", a=2)
            s2 = sinT[:].rearrange("p t (f a) -> p t f a", a=2)
            act.activation(c2[:, :, :, 0], cosr[:], ACT.Sin)
            act.activation(c2[:, :, :, 1], cosr[:], ACT.Sin)
            act.activation(s2[:, :, :, 1], red[:], ACT.Sin)
            act.activation(s2[:, :, :, 0], red[:], ACT.Sin, scale=-1.0).then_inc(sin_done, 1)
            act.activation(gates[:, 2:4], gates[:, 0:2], ACT.Tanh).then_inc(gates_ready, 1)

            def take_ctx(b):
                act.copy(ctxc[:], ctxall[:, bass.ds(b * TB, TB), :]).then_inc(ctxc_ready, 1)

            def do(region, b, name):
                if name in ("wout", "logit", "rank"):
                    return
                act.wait_ge(psx_full, use(region, b, name) + 1)
                if name in ("xnT", "ynT"):
                    act.copy(xT[:].rearrange("p c n -> p (c n)"), psX[:]).then_inc(psx_free, 1)
                elif name == "ctxT":
                    act.copy(ctxT[:], psX[:, 0:N]).then_inc(psx_free, 1)
                elif name == "q":
                    need(act, q_rot, b + 1)
                    act.copy(qsb[:], psX[:]).then_inc(psx_free, 1)
                elif name in ("kv0", "kv1"):
                    t = int(name[2])
                    act.copy(vstage[:, t, :], psX[:, D:2 * D]).then_inc(v_staged, 1)
                    need(act, k_rot, b + 1)
                    act.copy(ksb[:, t * D:(t + 1) * D], psX[:, 0:D]).then_inc(psx_free, 1)
                elif name == "attnT":
                    act.copy(attnT[:].rearrange("p c n -> p (c n)"), psX[:]).then_inc(psx_free, 1)

            def evac_qk(n, slot):
                act.wait_ge(t1_full, n + 1)
                act.copy(qk[:, slot, :], psT1[:]).then_inc(qk_ready, 1)

            def expo(b, g, j):
                act.wait_ge(st_full, b * H + 4 * g + j + 1)
                if j == 0:
                    need(act, pv_done, b * G + g - 1)
                act.activation(probs[:, g % 2, j * 2 * N:(j + 1) * 2 * N], psST[j % 2][:], ACT.Exp,
                               scale=SCALE).then_inc(exp_done, 1)

            def evac_ot(b, g):
                act.wait_ge(pv_done, b * G + g + 1)
                act.copy(otsb[:, g % 2, :], psO[:, 0:N]).then_inc(ot_ready, 1)

            def copy_v(b):
                act.wait_ge(v_staged, TB * (b + 1))
                act.copy(vaug[:].rearrange("p t (h c) -> p (t h) c", c=VCOLS)[:, :, 0:HD],
                         vstage[:].rearrange("p t (h d) -> p (t h) d", d=HD)).then_inc(v_ready, 1)

            def weights_of(b):
                act.wait_ge(nbest_ready, b)
                for t in range(TB):
                    last = act.activation(expl[:, t, :], logit[:, t, :], ACT.Exp, bias=nbest[:, t:t + 1])
                last.then_inc(expl_ready, 1)

            def step(region, b, g):
                one, two = item(region, b, g, 1), item(region, b, g, 2)
                new = region != "tail"
                jobs = jobs_at(region, g)
                if g == 0 and region in ("first", "middle"):
                    take_ctx(b + 1)
                if one:
                    expo(*one, 0)
                if jobs[0]:
                    do(region, b, jobs[0])
                if one:
                    for j in range(1, 4):
                        expo(*one, j)
                if jobs[1]:
                    do(region, b, jobs[1])
                if two:
                    evac_ot(*two)
                if new and g == 1:
                    copy_v(b)
                if new and g == 7 and region != "first":
                    weights_of(b)
                if new and g < G - 1:
                    evac_qk(b * G + g + 1, (g + 1) % 2)
                elif new and region != "last":
                    evac_qk(b * G + G, 0)

            act.wait_ge(ctx_in, 16)
            take_ctx(0)
            act.wait_ge(pads, 3)
            for name in prep:
                do("pro", -1, name)
            evac_qk(0, 0)

            def batch(region, b):
                for g in range(G):
                    step(region, b, g)

            regions(act, batch)
            for g in range(3):
                step("tail", B, g)
            do("tail", B, "attnT")
            do("tail", B, "ynT")
            weights_of(B)

            def silu(e, par):
                act.wait_ge(gu_full, e + 1)
                need(act, h_ready, e - 1)
                act.activation(sg[:, par, :], bank_gu[par][:, 0:I], ACT.Silu).then_inc(sg_ready, 1)

            def weigh(e, r, rounds):
                act.wait_ge(y_full, e + 1)
                need(act, acc_done[r % ACCS], 16 * (2 * rounds + r // ACCS - 1))
                act.activation(ye[:, r, :], bank_y[r % 2][:, 0:D], ACT.Copy,
                               scale=xe[:, r, bass.ds(D + e, 1)]).then_inc(ye_ready, 1)

            silu(0, 0)
            silu(1, 1)
            for r in range(RING):
                silu(r + 2, r % 2)
                weigh(r, r, 0)
            with act.Fori(1, E // RING - 1) as it:
                for r in range(RING):
                    silu(it * RING + r + 2, r % 2)
                    weigh(it * RING + r, r, it)
            for r in range(RING):
                e = E - RING + r
                if e + 2 < E:
                    silu(e + 2, r % 2)
                weigh(e, r, E // RING - 1)

        @block.vector
        def _(dve):
            LT = Links(dve, table_links, 0)
            dve.wait_ge(small_in, 64)
            freqs = [10000.0 ** (-f / HALF) for f in range(HALF)]
            a4 = ang[:].rearrange("p t (a f) -> p t a f", f=HALF)
            for f in range(HALF):
                last = dve.tensor_scalar(a4[:, :, :, f], pos[:], freqs[f], None, ALU.mult)
            LT.link(last)
            LT.link(dve.tensor_scalar(turns[:], ang[:], 1.0 / TWO_PI, MAGIC, ALU.mult, ALU.add))
            LT.link(dve.tensor_scalar(turns[:], turns[:], MAGIC, None, ALU.subtract))
            hi, rest1 = two_part(TWO_PI)
            LT.link(dve.scalar_tensor_tensor(red[:], turns[:], -hi, ang[:], ALU.mult, ALU.add))
            LT.link(dve.scalar_tensor_tensor(red[:], turns[:], -rest1, red[:], ALU.mult, ALU.add))
            LT.link(dve.tensor_scalar(cosr[:], red[:], TWO_PI / 4, None, ALU.add))
            LT.link(dve.tensor_scalar(over[:], cosr[:], PI_F, -TWO_PI, ALU.is_gt, ALU.mult))
            LT.link(dve.tensor_tensor(cosr[:], cosr[:], over[:], ALU.add))
            LT.link(dve.tensor_scalar(cosr[:], cosr[:], PI_F, -PI_F, ALU.min, ALU.max))
            dve.tensor_scalar(red[:], red[:], PI_F, -PI_F, ALU.min, ALU.max).then_inc(tables, 1)
            dve.wait_ge(rw_T, 1)
            dve.tensor_copy(wrT[:].rearrange("p c e -> p (c e)"), psO[:, 0:DC * E]).then_inc(wrT_ready, 1)

            dve.wait_ge(x_in, 16)
            with dve.Fori(0, NT) as t:
                dve.bn_stats(stat1[:, bass.ds(t, 1), :].rearrange("p a s -> p (a s)"),
                             xall[:, bass.ds(t, 1), :].rearrange("p a d -> p (a d)")).then_inc(stat_links, 1)
            dve.wait_ge(stat_links, NT)
            for t in range(NT):
                last = dve.bn_aggr(mv1[:, t, :], stat1[:, t, :])
            last.then_inc(stats1, 1)
            dve.wait_ge(rstd1_ready, 1)

            def normalise(b):
                for t in range(TB):
                    last = dve.tensor_scalar(xn[:, t, :], xall[:, bass.ds(b * TB + t, 1), :].rearrange("p a d -> p (a d)"),
                                             mv1[:, bass.ds(b * TB + t, 1), 0], rstd1[:, bass.ds(b * TB + t, 1)],
                                             ALU.subtract, ALU.mult)
                last.then_inc(xn_ready, 1)

            def split(b, what, part, links):
                src, dst = (qsb, qsp) if what == "q" else (ksb, ksp)
                size = TB * H * PARTS
                to = dst[:, bass.ds((b % 2) * size, size)].rearrange("p (n r d) -> p n r d", r=PARTS // HD, d=HD)
                v = src[:].rearrange("p (n d) -> p n d", d=HD)
                r = rest[:].rearrange("p (n d) -> p n d", d=HD)
                n = TB * H

                def spread(ap, k):
                    return ap.unsqueeze(2).to_broadcast([P, n, k, HD])

                if part == 0:
                    dve.wait_ge(q_rot if what == "q" else k_rot, b + 1)
                    if what == "q":
                        links.link(dve.tensor_copy(to[:, :, 0:3, :], spread(v, 3)))
                    else:
                        dve.tensor_copy(to[:, :, 4:6, :], spread(v, 2))
                        links.link(dve.tensor_copy(to[:, :, 0, :], v))
                elif part == 1:
                    links.link(dve.tensor_tensor(r, v, to[:, :, 0, :], ALU.subtract))
                elif part == 2:
                    links.link(dve.tensor_copy(to[:, :, 3:5, :] if what == "q" else to[:, :, 1:4:2, :], spread(r, 2)))
                else:
                    dve.tensor_tensor(to[:, :, 5 if what == "q" else 2, :], r, to[:, :, 3, :],
                                      ALU.subtract).then_inc(split_done, 1)

            SPLIT_LINKS = 6
            SPLIT = {4: [("q", 0), ("q", 1)], 5: [("q", 2), ("q", 3)], 6: [("k", 0), ("k", 1)], 7: [("k", 2), ("k", 3)]}

            def row_max(b, g, j):
                dve.wait_ge(s_full, b * H + 4 * g + j + 1)
                if j == 0:
                    need(dve, m_ready, b * G + g - 1)
                dve.tensor_reduce(nmax[:, g % 2, :, j], psS[j % 2][:].rearrange("p (t k) -> p t k", t=TB), AX.X, ALU.max,
                                  negate=True).then_inc(max_done, 1)

            def store_max(b, g):
                size = TB * H * PARTS
                to = qsp[:, bass.ds((b % 2) * size, size)].rearrange("p (t h r) -> p t h r", t=TB, r=PARTS)
                to = to[:, :, 4 * g:4 * g + 4, :]
                dve.wait_ge(max_done, b * H + 4 * g + 4)
                dve.tensor_copy(to[:, :, :, PROD], nmax[:, g % 2]).then_inc(mhi_done, 1)
                dve.wait_ge(mhi_done, b * G + g + 1)
                dve.tensor_tensor(to[:, :, :, PROD + 1], nmax[:, g % 2], to[:, :, :, PROD], ALU.subtract).then_inc(m_ready, 1)

            def evac_qm(b, g):
                dve.wait_ge(t2_full, b * G + g + 1)
                dve.tensor_copy(qm[:], psT2[:, 0:2 * N]).then_inc(qm_ready, 1)

            def norm(region, b, g, bi, gi):
                n = use(region, b, f"ot{g}")
                dve.wait_ge(psx_full, n + 1)
                o = psX[:, 0:2 * P].rearrange("p (t j c) -> p t j c", t=TB, j=4)
                dve.reciprocal(rden[:], o[:, :, :, DEN]).then_inc(rden_done, 1)
                dve.wait_ge(rden_done, bi * G + gi + 1)
                dve.tensor_tensor(attn[:, :, gi * 32:(gi + 1) * 32].rearrange("p t (j d) -> p t j d", d=HD),
                                  o[:, :, :, 0:HD], rden[:].unsqueeze(3).to_broadcast([P, TB, 4, HD]),
                                  ALU.mult).then_inc(psx_free, 1)

            LN_LINKS, ROUTE_LINKS = 2, 11

            def residual(region, b):
                n = use(region, b, "wout")
                mine = xall[:, bass.ds((b - 1) * TB, TB), :]
                dve.wait_ge(psx_full, n + 1)
                dve.scalar_tensor_tensor(mine, psX[:].rearrange("p (t d) -> p t d", t=TB), gates[:, 2:3], mine,
                                         ALU.mult, ALU.add).then_inc(psx_free, 1)
                hold(dve, psx_free, n + 1)
                L = Links(dve, ln_links, (b - 1) * LN_LINKS)
                for t in range(TB):
                    last = dve.bn_stats(stat2[:, t, :], xall[:, bass.ds((b - 1) * TB + t, 1), :].rearrange("p a d -> p (a d)"))
                L.link(last)
                for t in range(TB):
                    last = dve.bn_aggr(mv2[:, t, :], stat2[:, t, :])
                L.link(last)
                dve.tensor_scalar(mv2[:, :, 1], mv2[:, :, 1], 1e-5, None, ALU.add).then_inc(stats2, 1)

            def second_norm(b):
                dve.wait_ge(rstd2_ready, b)
                dve.wait_ge(rows_ready, b)
                for t in range(TB):
                    last = dve.tensor_scalar(ybuf[:, t, :], xall[:, bass.ds((b - 1) * TB + t, 1), :].rearrange("p a d -> p (a d)"),
                                             mv2[:, t, 0:1], rstd2[:, t:t + 1], ALU.subtract, ALU.mult)
                last.then_inc(y_ready, 1)

            def choose(region, b, L):
                n = use(region, b, "logit")
                dve.wait_ge(psx_full, n + 1)
                dve.tensor_copy(logit[:].rearrange("p t e -> p (t e)"), psX[:, 0:TB * E]).then_inc(psx_free, 1)
                hold(dve, psx_free, n + 1)
                for t in range(TB):
                    last = dve.max(best[:, t, :], logit[:, t, :])
                L.link(last)
                dve.tensor_scalar(nbest[:], best[:, :, 0], -1.0, None, ALU.mult).then_inc(nbest_ready, 1)
                for t in range(TB):
                    last = dve.match_replace(cut[:, t, :], best[:, t, :], logit[:, t, :], -3.0e38)
                L.link(last)
                L.link(dve.tensor_tensor(chosen[:], cut[:], logit[:], ALU.not_equal))
                dve.tensor_copy(chosenb[:], chosen[:]).then_inc(chosen_ready, 1)

            def assign(region, b, L):
                dve.wait_ge(expl_ready, b)
                L.link(dve.tensor_tensor(wbuf[:], expl[:], chosen[:], ALU.mult))
                L.link(dve.tensor_reduce(wsum[:], wbuf[:], AX.X, ALU.add))
                L.link(dve.reciprocal(wrec[:], wsum[:]))
                dve.tensor_tensor(wbuf[:], wbuf[:], wrec[:].unsqueeze(2).to_broadcast([P, TB, E]),
                                  ALU.mult).then_inc(w_ready, 1)
                n = use(region, b, "rank")
                dve.wait_ge(psx_full, n + 1)
                rank = psX[:, 0:TB * E].rearrange("p (t e) -> p t e", t=TB)
                dve.tensor_scalar(drop[:], rank, float(C), 2.0 * E * C, ALU.is_ge, ALU.mult)
                L.link(dve.tensor_tensor(place[:], rank, slot0[:].rearrange("p (t e) -> p t e", t=TB), ALU.add))
                dve.tensor_tensor(place[:], place[:], drop[:], ALU.max).then_inc(psx_free, 1)
                dve.wait_ge(psx_free, n + 1)
                L.link(dve.scalar_tensor_tensor(place[:], place[:], 1.0, chosen[:], ALU.add, ALU.mult))
                for t in range(TB):
                    last = dve.max(best8[:, t, :], place[:, t, :])
                L.link(last)
                need(dve, scattered, 16 * NSC * (b - 1))
                dve.tensor_scalar(idx[:], best8[:], 1.0, None, ALU.subtract).then_inc(idx_ready, 1)
                L.link(dve.tensor_tensor(seen[:], seen[:], chosenb[:, 0, :], ALU.add))
                L.link(dve.tensor_tensor(seen[:], seen[:], chosenb[:, 1, :], ALU.add))
                assert L.n == ROUTE_LINKS, L.n

            def step(region, b, g, links, route):
                one, three = item(region, b, g, 1), item(region, b, g, 3)
                new = region != "tail"
                jobs = jobs_at(region, g)
                if new:
                    row_max(b, g, 0)
                if one:
                    evac_qm(*one)
                if g == 0 and region in ("first", "middle"):
                    normalise(b + 1)
                if new:
                    row_max(b, g, 1)
                if "wout" in jobs:
                    residual(region, b)
                if new:
                    row_max(b, g, 2)
                if region in ("first", "middle"):
                    for what, part in SPLIT.get(g, [])[:1]:
                        split(b + 1, what, part, links)
                if new:
                    row_max(b, g, 3)
                    store_max(b, g)
                if region in ("first", "middle"):
                    for what, part in SPLIT.get(g, [])[1:]:
                        split(b + 1, what, part, links)
                if g == 5 and "ynT" in jobs:
                    second_norm(b)
                if "logit" in jobs:
                    choose(region, b, route)
                if "rank" in jobs:
                    assign(region, b, route)
                if three:
                    norm(region, b, g, *three)

            normalise(0)
            dve.wait_ge(gates_ready, 1)
            dve.wait_ge(pads, 3)
            links = Links(dve, split_links, 0)
            for what in ("q", "k"):
                for part in range(4):
                    split(0, what, part, links)
            assert links.n == SPLIT_LINKS, links.n

            def batch(region, b):
                links = Links(dve, split_links, (b + 1) * SPLIT_LINKS)
                route = Links(dve, route_links, (b - 1) * ROUTE_LINKS)
                for g in range(G):
                    step(region, b, g, links, route)

            regions(dve, batch)
            for g in range(3):
                step("tail", B, g, None, None)
            route = Links(dve, route_links, (B - 1) * ROUTE_LINKS)
            residual("tail", B)
            second_norm(B)
            choose("tail", B, route)
            assign("tail", B, route)

            def evac_xT(e, par):
                dve.wait_ge(xeT_full, e + 1)
                need(dve, gu_full, e - 1)
                dve.tensor_copy(xeT[:, par, :], bank_xT[par][:, 0:DC * C]).then_inc(xeT_ready, 1)

            def times_up(e, par):
                dve.wait_ge(sg_ready, e + 1)
                need(dve, hT_full, e - 1)
                dve.tensor_tensor(hsb[:, par, :], bank_gu[par][:, I:I2], sg[:, par, :], ALU.mult).then_inc(h_ready, 1)

            def evac_hT(e, par):
                dve.wait_ge(hT_full, e + 1)
                need(dve, y_full, e - 1)
                dve.tensor_copy(hT[0:I, par, :], bank_hT[par][0:I, 0:C]).then_inc(hT_ready, 1)

            def estep(s, k):
                known = isinstance(s, int)
                if not (known and s + 2 >= E):
                    evac_xT(s + 2, k % 2)
                if not (known and (s + 1 < 0 or s + 1 >= E)):
                    times_up(s + 1, (k + 1) % 2)
                if not (known and (s < 0 or s >= E)):
                    evac_hT(s, k % 2)

            for s in range(-2, 3):
                estep(s, s)
            LOOPS = (E - 5) // RING
            with dve.Fori(0, LOOPS) as it:
                for k in range(3, RING + 3):
                    estep(it * RING + k, k)
            for s in range(LOOPS * RING + 3, E + 1):
                estep(s, s)

            for a in range(ACCS):
                dve.wait_ge(fin_in[a], 32)
            L = Links(dve, fin_links, 0)
            for h in range(2):
                f = [fin[a][:, 4 * h:4 * h + 4, :] for a in range(ACCS)]
                dve.tensor_tensor(f[0], f[0], f[1], ALU.add)
                L.link(dve.tensor_tensor(f[2], f[2], f[3], ALU.add))
                L.link(dve.tensor_tensor(f[0], f[0], f[2], ALU.add))
                dve.scalar_tensor_tensor(xall[:, 4 * h:4 * h + 4, :], f[0], gates[:, 3:4], xall[:, 4 * h:4 * h + 4, :],
                                         ALU.mult, ALU.add).then_inc(out_ready, 1)

        @block.gpsimd
        def _(pool):
            pool.memset(zrow[:], 0.0).then_inc(pool_links, 1)
            pool.wait_ge(pool_links, 1)
            pool.iota(zrow[:, ID:ID + 1].bitcast(I32), [[0, 1]], base=T, channel_multiplier=1).then_inc(zrow_ready, 1)
            pool.memset(identf[:], 0.0).then_inc(pool_links, 1)
            pool.memset(before[:], 0.0).then_inc(pool_links, 1)
            pool.wait_ge(pool_links, 3)
            pool.affine_select(out=identf[:], in_=identf[:], compare_op=ALU.not_equal, fill=1.0, base=0,
                               pattern=[[-1, P]], channel_multiplier=1).then_inc(pool_links, 1)
            pool.affine_select(out=before[:], in_=before[:], compare_op=ALU.is_ge, fill=1.0, base=0,
                               pattern=[[-1, P]], channel_multiplier=1)
            pool.memset(onesb[:], 1.0)
            pool.memset(onesr[:], 1.0)
            pool.memset(seen[:], 0.0)
            pool.memset(half_neg[:], -0.5)
            pool.wait_ge(pool_links, 4)
            pool.tensor_copy(identb[:], identf[:]).then_inc(consts, 1)
            q16 = qsp[:].rearrange("p (n r) -> p n r", r=PARTS)
            k16 = ksp[:].rearrange("p (n r) -> p n r", r=PARTS)
            pool.memset(q16[:, :, PROD:PARTS].bitcast(F32), 0.0).then_inc(pads, 1)
            pool.memset(k16[:, :, MAXROWS:PARTS].bitcast(F32), 0.0)
            pool.memset(k16[:, :, PROD:MAXROWS], 1.0).then_inc(pads, 1)
            pool.memset(vaug[:], 0.0).then_inc(pool_links, 1)
            pool.wait_ge(pool_links, 5)
            pool.memset(vaug[:].rearrange("p t (h c) -> p (t h) c", c=VCOLS)[:, :, DEN:DEN + 1], 1.0).then_inc(pads, 1)
            pool.iota(ids[:], [[P, NT]], base=0, channel_multiplier=1)
            pool.iota(slot_i[:], [[0, TB], [C, E]], base=0, channel_multiplier=0).then_inc(pool_links, 1)
            pool.wait_ge(pool_links, 6)
            pool.tensor_copy(slot0[:], slot_i[:]).then_inc(pool_links, 1)
            pool.memset(rows[:, :, ID:ROW], 0.0).then_inc(rows_ready, 1)

            pool.wait_ge(stats1, 1)
            pool.tensor_scalar(rstd1[:], mv1[:, :, 1], 1e-5, None, ALU.add).then_inc(pool_links, 1)
            pool.wait_ge(pool_links, 8)
            pool.tensor_tensor(rstd1[:], rstd1[:], half_neg[:], ALU.pow).then_inc(rstd1_ready, 1)
            pool.wait_ge(sin_done, 1)

            def rotate(region, b, what):
                buf, done = (qsb, q_rot) if what == "q" else (ksb, k_rot)
                if what == "k":
                    pool.wait_ge(q_rot, b + 2)
                else:
                    need(pool, k_rot, b + 1)
                hold(pool, psx_free, use(region, b, "q" if what == "q" else "kv1") + 1)
                if what == "q":
                    hold(pool, split_done, 2 * b + 2)
                L = Links(pool, rope_links, (b + 1) * 2 + (0 if what == "q" else 1))
                n = [P, TB, H, HD]
                v = buf[:].rearrange("p (t h d) -> p t h d", t=TB, d=HD)
                a = rt[:].rearrange("p (t h d) -> p t h d", t=TB, d=HD)
                c = cosT[:, bass.ds((b + 1) * TB, TB), :].unsqueeze(2).to_broadcast(n)
                v2 = buf[:].rearrange("p (t h f a) -> p t (h f) a", t=TB, h=H, a=2)
                r2 = rt2[:].rearrange("p (t h f a) -> p t (h f) a", t=TB, h=H, a=2)
                pool.tensor_tensor(a, v, c, ALU.mult)
                for o in range(2):
                    s = sinT[:, bass.ds((b + 1) * TB, TB), o::2].unsqueeze(2).to_broadcast([P, TB, H, HD // 2])
                    vo = buf[:].rearrange("p (t h f a) -> p t h f a", t=TB, h=H, a=2)[:, :, :, :, 1 - o]
                    ro = rt2[:].rearrange("p (t h f a) -> p t h f a", t=TB, h=H, a=2)[:, :, :, :, o]
                    last = pool.tensor_tensor(ro, vo, s, ALU.mult)
                L.link(last)
                pool.tensor_tensor(buf[:], rt[:], rt2[:], ALU.add).then_inc(done, 1)

            def root(b):
                pool.wait_ge(stats2, b)
                pool.tensor_tensor(rstd2[:], mv2[:, :, 1], half_neg[:, 0:TB], ALU.pow).then_inc(rstd2_ready, 1)

            def scatter(b):
                need(pool, scattered, 16 * NSC * (b - 1))
                hold(pool, idx_ready, b)
                pool.tensor_copy(rows[:, :, 0:D], ybuf[:])
                pool.tensor_copy(rows[:, :, D:ID], wbuf[:])
                pool.tensor_copy(rows[:, :, ID].bitcast(I32), ids[:, bass.ds((b - 1) * TB, TB)]).then_inc(rows_ready, 1)
                hold(pool, rows_ready, b + 1)
                for t in range(TB):
                    for k in range(TOPK):
                        pool.indirect_dma_start(out=slots, out_offset=bass.IndirectOffsetOnAxis(ap=idx[:, t, k:k + 1], axis=0),
                                                in_=rows[:, t, :], in_offset=None, bounds_check=E * C - 1,
                                                oob_is_err=False).then_inc(scattered, 16)

            pool.wait_ge(slots_filled, 16)
            pool.wait_ge(acc_filled, 16 * ACCS)
            rotate("pro", -1, "q")
            rotate("pro", -1, "k")

            def batch(region, b):
                if region != "last":
                    rotate(region, b, "q")
                    rotate(region, b, "k")
                if region != "first":
                    root(b)
                    scatter(b)

            regions(pool, batch)
            root(B)
            scatter(B)

            def add_rows(e, r, rounds):
                pool.wait_ge(ye_ready, e + 1)
                hold(pool, acc_done[r % ACCS], 16 * (2 * rounds + r // ACCS))
                pool.indirect_dma_start(out=acc[r % ACCS],
                                        out_offset=bass.IndirectOffsetOnAxis(ap=xe[:, r, ID:ID + 1].bitcast(U32), axis=0),
                                        in_=ye[:, r, :], in_offset=None, bounds_check=T + P - 1, oob_is_err=True,
                                        compute_op=ALU.add).then_inc(acc_done[r % ACCS], 16)

            with pool.Fori(0, E // RING) as it:
                for r in range(RING):
                    add_rows(it * RING + r, r, it)


_INS = ["x", "ctx_1024", "fside_BxSx2_0", "g_xattn", "g_ffn", "L0_xattn_Wq", "L0_xattn_Wkv", "L0_xattn_Wout",
        "L0_xattn_bout", "L0_ffn_router_weight", "L0_ffn_gate_up_proj", "L0_ffn_down_proj"]


def kernel(**inputs):
    import numpy as _np
    import concourse.bacc as _bacc
    from concourse import mybir as _mybir
    from concourse.bass_utils import run_bass_kernel_spmd as _run

    nc = _bacc.Bacc("TRN2", target_bir_lowering=False, num_devices=1)
    arrays, args = {}, []
    for name in _INS:
        a = _np.ascontiguousarray(inputs[name])
        arrays[f"in_{name}"] = a
        args.append(nc.dram_tensor(f"in_{name}", a.shape, _mybir.dt.from_np(a.dtype), kind="ExternalInput").ap())
    shape = inputs["x"].shape
    out = nc.dram_tensor("out_0", shape, _mybir.dt.float32, kind="ExternalOutput").ap()
    flamingo(nc, *args, out)
    r = _run(nc, [arrays], core_ids=[0])
    return r.results[0]["out_0"]
```

```python
from contextlib import ExitStack

import concourse.bass as bass
from concourse import mybir

P = 128
F32 = mybir.dt.float32
BF16 = mybir.dt.bfloat16
U32 = mybir.dt.uint32
I32 = mybir.dt.int32
ALU = mybir.AluOpType
ACT = mybir.ActivationFunctionType
AX = mybir.AxisListType

PARTS = 64
PROD = 48
MAXROWS = 50
VCOLS = 32
LAG = 3
DEN = 8
ACCS = 4
RING = 16
CHUNK = 2
TOPK = 8
TWO_PI = 6.283185307179586
PI_F = 3.1415925
MAGIC = 12582912.0


def need(eng, sem, value):
    if isinstance(value, int) and value <= 0:
        return
    eng.wait_ge(sem, value)


def hold(eng, sem, value):
    eng.wait_ge(sem, value)
    eng.nop(nofuse=True)


class Links:

    def __init__(self, eng, sem, base):
        self.eng, self.sem, self.base, self.n = eng, sem, base, 0

    def link(self, ins):
        self.n += 1
        ins.then_inc(self.sem, 1)
        hold(self.eng, self.sem, self.base + self.n)


def two_part(v):
    hi = float(int(v * 256)) / 256
    return hi, v - hi


def flamingo(nc, x, ctx_1024, fside_BxSx2_0, g_xattn, g_ffn, L0_xattn_Wq, L0_xattn_Wkv, L0_xattn_Wout,
             L0_xattn_bout, L0_ffn_router_weight, L0_ffn_gate_up_proj, L0_ffn_down_proj, out):
    B, N, D = x.shape
    CD = ctx_1024.shape[2]
    HD = 8
    H = D // HD
    T = B * N
    NT = T // P
    TB = N // P
    G = H // 4
    E, _, I2 = L0_ffn_gate_up_proj.shape
    I = I2 // 2
    C = P
    DC = D // P
    ROW = D + E + 4
    ID = D + E
    ITEMS = B * G
    SCALE = float(HD) ** -0.5
    NSC = TB * TOPK
    HALF = HD // 4
    LATE = E // 4
    assert (N, D, CD, H, E, I, TB, G, DC, HALF) == (256, 256, 128, 32, 64, 96, 2, 8, 2, 2)

    xf = x.rearrange("b n d -> (b n) d").rearrange("(t p) d -> p t d", p=P)
    of = out.rearrange("b n d -> (b n) d").rearrange("(t p) d -> p t d", p=P)
    ctxf = ctx_1024.rearrange("b n d -> (b n) d").rearrange("(t p) d -> p t d", p=P)
    posf = fside_BxSx2_0.rearrange("b n d -> (b n) d").rearrange("(t p) d -> p t d", p=P)
    wgu_src = L0_ffn_gate_up_proj.rearrange("e (p c) f -> p e (c f)", c=DC)
    wd_src = L0_ffn_down_proj.rearrange("e i h -> i e h")

    slots = nc.dram_tensor("slots", [E * C, ROW], F32, kind="Internal").ap()
    acc = [nc.dram_tensor(f"acc{a}", [T + P, D], F32, kind="Internal").ap() for a in range(ACCS)]

    with ExitStack() as ctx:
        arena = (nc.sbuf_base + 63) // 64 * 64
        top = [arena]

        def at(name, shape, dt, offset):
            return nc.alloc_sbuf_tensor_at(name, shape, dt, offset=offset)

        def sb(name, shape, dt):
            n = 4 if dt != BF16 else 2
            for s in shape[1:]:
                n *= s
            here = top[0]
            top[0] = (here + n + 31) // 32 * 32
            return at(name, shape, dt, here)

        def sem(name):
            return ctx.enter_context(nc.semaphore(name))

        def psum(name, shape, dt):
            return ctx.enter_context(nc.psum_tensor(name, shape, dt))

        wd = sb("wd", [P, E, D], F32)
        gu_base = top[0]
        wgu = sb("wgu", [P, E, DC * I2], F32)
        late = gu_base + LATE * DC * I2 * 4
        end_of_weights = top[0]
        top[0] = late
        qsp = sb("qsp", [P, 2 * TB * H * PARTS], BF16)
        ksp = sb("ksp", [P, 2 * TB * H * PARTS], BF16)
        probs = sb("probs", [P, 2, 4 * 2 * N], F32)
        vaug = sb("vaug", [P, TB, H * VCOLS], F32)
        qk = sb("qk", [P, 4, 4 * N], BF16)
        qm = sb("qm", [P, 2, 2 * N], BF16)
        qsb = sb("qsb", [P, TB * D], F32)
        ksb = sb("ksb", [P, TB * D], F32)
        assert top[0] <= end_of_weights, (top[0], end_of_weights)
        top[0] = end_of_weights
        xall = sb("xall", [P, NT, D], F32)
        identf = sb("identf", [P, P], F32)
        identb = sb("identb", [P, P], BF16)
        before = sb("before", [P, P], BF16)
        onesb = sb("onesb", [P, P], BF16)
        boutg = sb("boutg", [P, D], F32)
        slot0 = sb("slot0", [P, TB * E], F32)
        slot_i = sb("slot_i", [P, TB * E], I32)
        ids = sb("ids", [P, NT], I32)
        half_neg = sb("half_neg", [P, NT], F32)
        gates = sb("gates", [P, 4], F32)
        wrT = sb("wrT", [P, DC, E], F32)
        stat2 = sb("stat2", [P, TB, 6], F32)
        mv2 = sb("mv2", [P, TB, 2], F32)
        rstd2 = sb("rstd2", [P, TB], F32)
        wbuf = sb("wbuf", [P, TB, E], F32)
        rows = sb("rows", [P, TB, ROW], F32)
        idx = sb("idx", [P, TB, TOPK], U32)
        logit = sb("logit", [P, TB, E], F32)
        best = sb("best", [P, TB, 8], F32)
        nbest = sb("nbest", [P, TB], F32)
        cut = sb("cut", [P, TB, E], F32)
        chosen = sb("chosen", [P, TB, E], F32)
        chosenb = sb("chosenb", [P, TB, E], BF16)
        zeros = sb("zeros", [P, 2], BF16)
        seen = sb("seen", [P, E], BF16)
        expl = sb("expl", [P, TB, E], F32)
        wsum = sb("wsum", [P, TB], F32)
        wrec = sb("wrec", [P, TB], F32)
        place = sb("place", [P, TB, E], F32)
        drop = sb("drop", [P, TB, E], F32)
        best8 = sb("best8", [P, TB, TOPK], F32)
        shared = top[0]
        rt = sb("rt", [P, TB * D], F32)
        vstage = sb("vstage", [P, TB, D], F32)
        rt2 = sb("rt2", [P, TB * D], F32)
        rest = sb("rest", [P, TB * D], F32)
        xn = sb("xn", [P, TB, D], F32)
        ctxc = sb("ctxc", [P, TB, CD], F32)
        ctxT = sb("ctxT", [P, N], F32)
        wq = sb("wq", [P, DC * D], F32)
        wkv = sb("wkv", [P, 2 * D], F32)
        otsb = sb("otsb", [P, 2, N], F32)
        attn = sb("attn", [P, TB, D], F32)
        attnT = sb("attnT", [P, DC, N], F32)
        xT = sb("xT", [P, DC, N], F32)
        wout = sb("wout", [P, DC * D], F32)
        pos = sb("pos", [P, NT, 2], F32)
        cosT = sb("cosT", [P, NT, HD], F32)
        sinT = sb("sinT", [P, NT, HD], F32)
        nmax = sb("nmax", [P, 2, TB, 4], F32)
        rden = sb("rden", [P, TB, 4], F32)
        stat1 = sb("stat1", [P, NT, 6], F32)
        mv1 = sb("mv1", [P, NT, 2], F32)
        rstd1 = sb("rstd1", [P, NT], F32)
        end_attn = top[0]
        print('ATT',end_attn, nc.sbuf_usable_end, shared)
        assert end_attn <= nc.sbuf_usable_end, (end_attn, nc.sbuf_usable_end)
        top[0] = shared
        xe = sb("xe", [P, RING, ROW], F32)
        ye = sb("ye", [P, ACCS, D], F32)
        xeT = sb("xeT", [P, 2, DC * C], F32)
        hsb = sb("hsb", [P, 2, I], F32)
        sg = sb("sg", [P, 2, I], F32)
        hT = sb("hT", [P, 2, C], F32)
        assert top[0] <= nc.sbuf_usable_end
        print('EXP',top[0])
        fin = [at(f"fin{a}", [P, NT, D], F32, arena + a * NT * D * 4) for a in range(ACCS)]
        ctxall = at("ctxall", [P, NT, CD], F32, late - 4 * NT * CD)
        rw = at("rw", [E, D], F32, late - 4 * NT * CD - 4 * D)
        ang_at = late - 4 * NT * CD - 4 * D - 6 * NT * 4 * 4
        ang, turns, red, cosr, over = (at(f"angle{i}", [P, NT, 4], F32, ang_at + i * NT * 4 * 4) for i in range(5))
        zrow = at("zrow", [P, ROW], F32, (ang_at - 4 * ROW) // 32 * 32)
        early = LATE - 8

        psT1 = psum("psT1", [P, 4 * N], BF16)
        psT2 = psum("psT2", [P, 4 * N], BF16)
        psS = [psum(f"psS{i}", [P, 2 * N], F32) for i in range(2)]
        psST = [psum(f"psST{i}", [P, 2 * N], F32) for i in range(2)]
        psO = psum("psO", [P, 2 * N], F32)
        psX = psum("psX", [P, 2 * N], F32)
        ps_ot = psO[:, N:2 * N]
        bank_xT = [psS[0], psS[1]]
        bank_gu = [psST[0], psST[1]]
        bank_hT = [psO, psX]
        bank_y = [psT1[:, :].bitcast(F32), psT2[:, :].bitcast(F32)]

        x_in, ctx_in, small_in, wproj_in = sem("x_in"), sem("ctx_in"), sem("small_in"), sem("wproj_in")
        wd_in = [sem(f"wd_in{i}") for i in range(4)]
        wgu_in = [sem(f"wgu_in{i}") for i in range(LATE // 8)]
        wgu_late = sem("wgu_late")
        acc_done = [sem(f"acc_done{a}") for a in range(ACCS)]
        slots_filled, acc_filled = sem("slots_filled"), sem("acc_filled")
        consts, zrow_ready = sem("consts"), sem("zrow_ready")
        table_links, sin_done, tables = sem("table_links"), sem("sin_done"), sem("tables")
        rw_T, wrT_ready = sem("rw_T"), sem("wrT_ready")
        stats1, rstd1_ready, gates_ready = sem("stats1"), sem("rstd1_ready"), sem("gates_ready")
        stat_links = sem("stat_links")
        xn_ready, ctxc_ready = sem("xn_ready"), sem("ctxc_ready")
        psx_full, psx_free = sem("psx_full"), sem("psx_free")
        v_staged = sem("v_staged")
        q_rot, k_rot, rope_links = sem("q_rot"), sem("k_rot"), sem("rope_links")
        split_links, split_done = sem("split_links"), sem("split_done")
        pads = sem("pads")
        t1_full, qk_ready = sem("t1_full"), sem("qk_ready")
        s_full, max_done, mhi_done, m_ready = sem("s_full"), sem("max_done"), sem("mhi_done"), sem("m_ready")
        t2_full, qm_ready = sem("t2_full"), sem("qm_ready")
        st_full, exp_done, pv_done = sem("st_full"), sem("exp_done"), sem("pv_done")
        ot_ready, rden_done, v_ready = sem("ot_ready"), sem("rden_done"), sem("v_ready")
        ot_turned, normed, biased = sem("ot_turned"), sem("normed"), sem("biased")
        x1_ready, stats2, rstd2_ready, y_ready = sem("x1_ready"), sem("stats2"), sem("rstd2_ready"), sem("y_ready")
        ln_links, route_links = sem("ln_links"), sem("route_links")
        nbest_ready, expl_ready, chosen_ready, idx_ready = (
            sem("nbest_ready"), sem("expl_ready"), sem("chosen_ready"), sem("idx_ready"))
        seen_done = sem("seen_done")
        rows_ready = sem("rows_ready")
        scattered = sem("scattered")
        xe_in = [sem(f"xe_in{i}") for i in range(RING)]
        xeT_full, xeT_ready, gu_full, sg_ready, h_ready = (
            sem("xeT_full"), sem("xeT_ready"), sem("gu_full"), sem("sg_ready"), sem("h_ready"))
        hT_full, hT_ready, y_full, ye_ready = sem("hT_full"), sem("hT_ready"), sem("y_full"), sem("ye_ready")
        fin_in = [sem(f"fin_in{a}") for a in range(ACCS)]
        pool_links = sem("pool_links")
        fin_links, out_ready, out_done = sem("fin_links"), sem("out_ready"), sem("out_done")

        prep = ["ctxT", "xnT", "q", "kv0", "kv1"]
        SLOT = {0: ("ctxT", None, "xnT"), 1: ("q_a", None, "q"), 2: (None, None, "kv0"), 3: ("kv1", "attnT", "wout_a"),
                4: ("wout", None, None), 5: (None, None, "ynT"), 6: ("logit", None, None), 7: ("rank", None, None)}
        epi = ["attnT", "wout", "ynT", "logit", "rank"]

        def jobs_of(names):
            return [name for g in range(G) for name in SLOT[g] if name in names]

        FIRST, MIDDLE, LAST, TAIL = jobs_of(prep), jobs_of(prep + epi), jobs_of(epi), epi
        BASE1 = len(prep) + len(FIRST)
        BASE_LAST = BASE1 + (B - 2) * len(MIDDLE)
        BASE_TAIL = BASE_LAST + len(LAST)

        def use(region, b, name):
            if region == "pro":
                return prep.index(name)
            if region == "first":
                return len(prep) + FIRST.index(name)
            if region == "middle":
                return BASE1 + (b - 1) * len(MIDDLE) + MIDDLE.index(name)
            if region == "last":
                return BASE_LAST + LAST.index(name)
            return BASE_TAIL + TAIL.index(name)

        def jobs_at(region, g):
            has = {"first": prep, "middle": prep + epi, "last": epi, "tail": []}[region]
            return [n if n and n.removesuffix("_a") in has else None for n in SLOT[g]]

        def item(region, b, g, back):
            if region == "tail" and g >= back:
                return None
            if g >= back:
                return b, g - back
            return None if region == "first" else (b - 1, g - back + G)

        def regions(eng, body):
            body("first", 0)
            with eng.Fori(1, B - 1) as b:
                body("middle", b)
            body("last", B - 1)

        def qm_by_act(region, g):
            return g >= 4 and region != "tail"

        block = ctx.enter_context(nc.Block())

        @block.sync
        def _(sp):
            sp.dma_start(xall[:], xf).then_inc(x_in, 16)
            sp.dma_start(pos[:], posf).then_inc(small_in, 16)
            sp.dma_start(wq[:], L0_xattn_Wq.rearrange("(p c) n -> p (c n)", c=DC)).then_inc(wproj_in, 16)
            sp.dma_start(ctxall[:], ctxf).then_inc(ctx_in, 16)
            sp.dma_start(wkv[:], L0_xattn_Wkv).then_inc(wproj_in, 16)
            sp.dma_start(rw[:], L0_ffn_router_weight).then_inc(small_in, 16)
            sp.dma_start(gates[:, 0:1], g_xattn.partition_broadcast(P)).then_inc(small_in, 16)
            sp.dma_start(gates[:, 1:2], g_ffn.partition_broadcast(P)).then_inc(small_in, 16)
            sp.dma_start(wout[:], L0_xattn_Wout.rearrange("(p c) n -> p (c n)", c=DC)).then_inc(wproj_in, 16)
            sp.dma_start(boutg[:], L0_xattn_bout.partition_broadcast(P)).then_inc(wproj_in, 16)
            sp.wait_ge(zrow_ready, 1)
            sp.dma_start(slots.rearrange("(e c) r -> c e r", c=C),
                         zrow[:].unsqueeze(1).to_broadcast([P, E, ROW])).then_inc(slots_filled, 16)
            for i in range(4):
                n = E // 4
                sp.dma_start(wd[0:I, i * n:(i + 1) * n, :], wd_src[:, i * n:(i + 1) * n, :]).then_inc(wd_in[i], 16)
            for a in range(ACCS):
                sp.dma_start(acc[a].rearrange("(t p) d -> p t d", p=P),
                             zrow[:, 0:D].unsqueeze(1).to_broadcast([P, NT + 1, D])).then_inc(acc_filled, 16)

            def load_gu(i):
                sp.dma_start(wgu[:, 8 * i:8 * i + 8, :], wgu_src[:, 8 * i:8 * i + 8, :]).then_inc(wgu_in[i], 16)

            for i in range(early // 8):
                load_gu(i)
            sp.wait_ge(ctxc_ready, B)
            sp.wait_ge(wrT_ready, 1)
            sp.wait_ge(tables, 1)
            sp.wait_ge(slots_filled, 16)
            sp.wait_ge(acc_filled, 16 * ACCS)
            load_gu(early // 8)
            sp.wait_ge(pv_done, ITEMS)
            sp.wait_ge(qm_ready, ITEMS)
            for e in range(LATE, E, CHUNK):
                sp.dma_start(wgu[:, e:e + CHUNK, :], wgu_src[:, e:e + CHUNK, :]).then_inc(wgu_late, 16)
            sp.wait_ge(scattered, 16 * NSC * B)

            def load_slots(e, r):
                sp.dma_start(xe[:, r, :], slots[bass.ds(e * C, C), :]).then_inc(xe_in[r], 16)

            for r in range(RING):
                load_slots(r, r)
            with sp.Fori(1, E // RING) as it:
                for r in range(RING):
                    sp.wait_ge(acc_done[r % ACCS], 16 * ((RING // ACCS) * (it - 1) + r // ACCS + 1))
                    load_slots(it * RING + r, r)
            for a in range(ACCS):
                sp.wait_ge(acc_done[a], 16 * (E // ACCS))
                for h in range(2):
                    sp.dma_start(fin[a][:, h * 4:h * 4 + 4, :],
                                 acc[a].rearrange("(t p) d -> p t d", p=P)[:, h * 4:h * 4 + 4, :]).then_inc(fin_in[a], 16)
            for h in range(2):
                sp.wait_ge(out_ready, h + 1)
                sp.dma_start(of[:, h * 4:h * 4 + 4, :], xall[:, h * 4:h * 4 + 4, :]).then_inc(out_done, 16)
            sp.wait_ge(out_done, 32)

        @block.tensor
        def _(pe):
            pe.wait_ge(consts, 1)
            pe.wait_ge(small_in, 64)

            def bank_x(region, b, name):
                need(pe, psx_free, use(region, b, name))

            for c in range(DC):
                last = pe.transpose(psO[:, c * E:(c + 1) * E], rw[:, c::DC], identf[0:E, 0:E])
            last.then_inc(rw_T, 1)

            def do(region, b, name):
                name, _, half = name.partition("_")
                bank_x(region, b, name)
                tiles = (0,) if half else (1,) if region not in ("pro", "tail") else range(TB)
                if name == "xnT":
                    pe.wait_ge(xn_ready, TB * (b + 2))
                    for t in range(TB):
                        for c in range(DC):
                            last = pe.transpose(psX[:, (c * TB + t) * P:(c * TB + t + 1) * P], xn[:, t, c::DC], identf[:])
                elif name == "ctxT":
                    pe.wait_ge(ctxc_ready, b + 2)
                    for t in range(TB):
                        last = pe.transpose(psX[:, t * P:(t + 1) * P], ctxc[:, t, :], identf[:])
                elif name == "q":
                    for t in tiles:
                        for c in range(DC):
                            last = pe.matmul(psX[:, t * D:(t + 1) * D], xT[:, c, t * P:(t + 1) * P],
                                             wq[:, c * D:(c + 1) * D], start=(c == 0), stop=(c == DC - 1))
                elif name in ("kv0", "kv1"):
                    t = int(name[2])
                    last = pe.matmul(psX[:, 0:2 * D], ctxT[:, t * P:(t + 1) * P], wkv[:], start=True, stop=True)
                elif name == "attnT":
                    pe.wait_ge(normed, b * G)
                    for t in range(TB):
                        for c in range(DC):
                            last = pe.transpose(psX[:, (c * TB + t) * P:(c * TB + t + 1) * P], attn[:, t, c::DC], identf[:])
                elif name == "wout":
                    for t in tiles:
                        for c in range(DC):
                            last = pe.matmul(psX[:, t * D:(t + 1) * D], attnT[:, c, t * P:(t + 1) * P],
                                             wout[:, c * D:(c + 1) * D], start=(c == 0), stop=(c == DC - 1))
                elif name == "ynT":
                    pe.wait_ge(y_ready, TB * b)
                    for t in range(TB):
                        for c in range(DC):
                            last = pe.transpose(psX[:, (c * TB + t) * P:(c * TB + t + 1) * P], rows[:, t, c:D:DC], identf[:])
                elif name == "logit":
                    for t in range(TB):
                        for c in range(DC):
                            last = pe.matmul(psX[:, t * E:(t + 1) * E], xT[:, c, t * P:(t + 1) * P], wrT[:, c, :],
                                             start=(c == 0), stop=(c == DC - 1))
                elif name == "rank":
                    pe.wait_ge(chosen_ready, b)
                    pe.matmul(psX[:, 0:E], before[:], chosenb[:, 0, :], start=True, stop=False)
                    pe.matmul(psX[:, 0:E], onesb[:], seen[:], start=False, stop=True)
                    pe.matmul(psX[:, E:2 * E], before[:], chosenb[:, 1, :], start=True, stop=False)
                    pe.matmul(psX[:, E:2 * E], onesb[:], chosenb[:, 0, :], start=False, stop=False)
                    last = pe.matmul(psX[:, E:2 * E], onesb[:], seen[:], start=False, stop=True)
                if not half:
                    last.then_inc(psx_full, 1)

            def t1(b, g, par):
                if g == 0:
                    pe.wait_ge(split_done, 2 * (b + 1))
                need(pe, qk_ready, b * G + g)
                for src, o in ((qsp, 0), (ksp, 2 * N)):
                    for ct in range(2):
                        for t in range(TB):
                            col = par * (TB * H * PARTS) + t * H * PARTS + (4 * g + 2 * ct) * PARTS
                            last = pe.transpose(psT1[:, o + ct * N + t * P:o + ct * N + (t + 1) * P],
                                                src[:, bass.ds(col, P)], identb[:])
                last.then_inc(t1_full, 1)

            def logits(b, g, j):
                a, ct = 64 * (j % 2), j // 2
                need(pe, max_done, b * H + 4 * g + j - 1)
                for t in range(TB):
                    last = pe.matmul(psS[j % 2][:, t * N:(t + 1) * N],
                                     qk[a:a + PARTS, g % 4, ct * N + t * P:ct * N + (t + 1) * P],
                                     qk[a:a + PARTS, g % 4, 2 * N + ct * N:2 * N + (ct + 1) * N], start=True, stop=True)
                last.then_inc(s_full, 1)

            def t2(b, g, par):
                hold(pe, m_ready, b * G + g + 1)
                for ct in range(2):
                    for t in range(TB):
                        col = par * (TB * H * PARTS) + t * H * PARTS + (4 * g + 2 * ct) * PARTS
                        last = pe.transpose(psT2[:, ct * N + t * P:ct * N + (t + 1) * P],
                                            qsp[:, bass.ds(col, P)], identb[:])
                last.then_inc(t2_full, 1)

            def shifted(b, g, j):
                a, ct = 64 * (j % 2), j // 2
                if j == 0:
                    pe.wait_ge(qm_ready, b * G + g + 1)
                need(pe, exp_done, b * H + 4 * g + j - 1)
                for kc in range(TB):
                    last = pe.matmul(psST[j % 2][:, kc * N:(kc + 1) * N],
                                     qk[a:a + PARTS, g % 4, 2 * N + ct * N + kc * P:2 * N + ct * N + (kc + 1) * P],
                                     qm[a:a + PARTS, g % 2, ct * N:(ct + 1) * N], start=True, stop=True)
                last.then_inc(st_full, 1)

            def pv(b, g):
                pe.wait_ge(exp_done, b * H + 4 * g + 4)
                need(pe, normed, b * G + g)
                if g == 0:
                    pe.wait_ge(v_ready, b + 1)
                for kc in range(TB):
                    for j in range(4):
                        last = pe.matmul(psO[32 * j:32 * j + 32, 0:N],
                                         vaug[:, kc, (4 * g + j) * VCOLS:(4 * g + j + 1) * VCOLS],
                                         probs[:, g % 2, (2 * j + kc) * N:(2 * j + kc + 1) * N],
                                         start=(kc == 0), stop=(kc == TB - 1))
                last.then_inc(pv_done, 1)

            def ot(b, g):
                pe.wait_ge(ot_ready, b * G + g + 1)
                for t in range(TB):
                    last = pe.transpose(ps_ot[:, t * P:(t + 1) * P], otsb[:, g % 2, t * P:(t + 1) * P], identf[:])
                last.then_inc(ot_turned, 1)

            def step(region, b, g):
                one, two, three = (item(region, b, g, back) for back in range(1, LAG + 1))
                new = region != "tail"
                jobs = jobs_at(region, g)
                if new:
                    pe.wait_ge(qk_ready, b * G + g + 1)
                    logits(b, g, 0)
                    logits(b, g, 1)
                if one:
                    if two:
                        pe.wait_ge(qm_ready, two[0] * G + two[1] + 1)
                    t2(*one, one[0] % 2)
                if new and g < G - 1:
                    t1(b, g + 1, b % 2)
                if jobs[0]:
                    do(region, b, jobs[0])
                if new:
                    logits(b, g, 2)
                if two:
                    shifted(*two, 0)
                if new:
                    logits(b, g, 3)
                if two:
                    shifted(*two, 1)
                if new and g == G - 1 and region != "last":
                    t1(b + 1, 0, (b + 1) % 2)
                if jobs[1]:
                    do(region, b, jobs[1])
                if three:
                    pv(*three)
                if two:
                    shifted(*two, 2)
                    shifted(*two, 3)
                if three:
                    ot(*three)
                if jobs[2]:
                    do(region, b, jobs[2])

            pe.wait_ge(wproj_in, 64)
            pe.wait_ge(wrT_ready, 1)
            for name in prep:
                do("pro", -1, name)
            pe.wait_ge(pads, 3)
            t1(0, 0, 0)

            def batch(region, b):
                for g in range(G):
                    step(region, b, g)

            regions(pe, batch)
            for g in range(LAG):
                step("tail", B, g)
            for name in epi:
                do("tail", B, name)

            pe.wait_ge(psx_free, BASE_TAIL + len(TAIL))
            for s in (*wd_in, *wgu_in):
                pe.wait_ge(s, 16)
            pe.wait_ge(wgu_late, 16 * (E - LATE) // CHUNK)

            def to_cols(e, par, r, rounds):
                pe.wait_ge(xe_in[r], 16 * rounds)
                need(pe, xeT_ready, e - 1)
                for c in range(DC):
                    last = pe.transpose(bank_xT[par][:, c * C:(c + 1) * C], xe[:, r, c:D:DC], identf[:])
                last.then_inc(xeT_full, 1)

            def gate_up(e, par):
                pe.wait_ge(xeT_ready, e + 1)
                need(pe, h_ready, e - 1)
                for c in range(DC):
                    last = pe.matmul(bank_gu[par][:, 0:I2], xeT[:, par, c * C:(c + 1) * C],
                                     wgu[:, e, c * I2:(c + 1) * I2], start=(c == 0), stop=(c == DC - 1))
                last.then_inc(gu_full, 1)

            def turn_h(e, par):
                pe.wait_ge(h_ready, e + 1)
                need(pe, hT_ready, e - 1)
                pe.transpose(bank_hT[par][0:I, 0:C], hsb[:, par, :], identf[:]).then_inc(hT_full, 1)

            def down(e, par):
                pe.wait_ge(hT_ready, e + 1)
                need(pe, ye_ready, e - 1)
                pe.matmul(bank_y[par][:, 0:D], hT[0:I, par, :], wd[0:I, e, :], start=True, stop=True).then_inc(y_full, 1)

            def estep(s, k, it=0):
                first, final = isinstance(s, int) and s < 1, isinstance(s, int) and s > E - 3
                if not final:
                    e = s + 2
                    to_cols(e, k % 2, (k + 2) % RING, it + (k + 2) // RING + 1)
                if not (isinstance(s, int) and (s + 1 < 0 or s + 1 >= E)):
                    gate_up(s + 1, (k + 1) % 2)
                if not (isinstance(s, int) and (s < 0 or s >= E)):
                    turn_h(s, k % 2)
                if not first:
                    down(s - 1, (k + 1) % 2)

            LOOPS = (E - 5) // RING
            for s in range(-2, 3):
                estep(s, s)
            with pe.Fori(0, LOOPS) as it:
                for k in range(3, RING + 3):
                    estep(it * RING + k, k, it)
            for s in range(LOOPS * RING + 3, E + 1):
                estep(s, s)

        @block.scalar
        def _(act):
            act.wait_ge(small_in, 64)
            act.wait_ge(tables, 1)
            c2 = cosT[:].rearrange("p t (f a) -> p t f a", a=2)
            s2 = sinT[:].rearrange("p t (f a) -> p t f a", a=2)
            act.activation(c2[:, :, :, 0], cosr[:], ACT.Sin)
            act.activation(c2[:, :, :, 1], cosr[:], ACT.Sin)
            act.activation(s2[:, :, :, 1], red[:], ACT.Sin)
            act.activation(s2[:, :, :, 0], red[:], ACT.Sin, scale=-1.0).then_inc(sin_done, 1)
            act.activation(gates[:, 2:4], gates[:, 0:2], ACT.Tanh).then_inc(gates_ready, 1)

            def take_ctx(b):
                act.copy(ctxc[:], ctxall[:, bass.ds(b * TB, TB), :]).then_inc(ctxc_ready, 1)

            def do(region, b, name):
                if name in (None, "q_a", "wout_a", "wout", "logit", "rank"):
                    return
                act.wait_ge(psx_full, use(region, b, name) + 1)
                if name in ("xnT", "ynT"):
                    act.copy(xT[:].rearrange("p c n -> p (c n)"), psX[:]).then_inc(psx_free, 1)
                elif name == "ctxT":
                    act.copy(ctxT[:], psX[:, 0:N]).then_inc(psx_free, 1)
                elif name == "q":
                    need(act, q_rot, b + 1)
                    act.copy(qsb[:], psX[:]).then_inc(psx_free, 1)
                elif name in ("kv0", "kv1"):
                    t = int(name[2])
                    need(act, v_ready, b + 1)
                    act.copy(vstage[:, t, :], psX[:, D:2 * D]).then_inc(v_staged, 1)
                    need(act, k_rot, b + 1)
                    act.copy(ksb[:, t * D:(t + 1) * D], psX[:, 0:D]).then_inc(psx_free, 1)
                elif name == "attnT":
                    act.copy(attnT[:].rearrange("p c n -> p (c n)"), psX[:]).then_inc(psx_free, 1)

            def evac_qk(n, slot):
                act.wait_ge(t1_full, n + 1)
                act.copy(qk[:, slot, :], psT1[:]).then_inc(qk_ready, 1)

            def expo(b, g, j):
                act.wait_ge(st_full, b * H + 4 * g + j + 1)
                if j == 0:
                    need(act, pv_done, b * G + g - 1)
                act.activation(probs[:, g % 2, j * 2 * N:(j + 1) * 2 * N], psST[j % 2][:], ACT.Exp,
                               scale=SCALE).then_inc(exp_done, 1)

            def evac_qm(b, g):
                act.wait_ge(t2_full, b * G + g + 1)
                act.copy(qm[:, g % 2, :], psT2[:, 0:2 * N]).then_inc(qm_ready, 1)

            def evac_ot(b, g):
                act.wait_ge(pv_done, b * G + g + 1)
                act.copy(otsb[:, g % 2, :], psO[:, 0:N]).then_inc(ot_ready, 1)

            def copy_v(b):
                act.wait_ge(v_staged, TB * (b + 1))
                act.copy(vaug[:].rearrange("p t (h c) -> p (t h) c", c=VCOLS)[:, :, 0:HD],
                         vstage[:].rearrange("p t (h d) -> p (t h) d", d=HD)).then_inc(v_ready, 1)

            def weights_of(b):
                act.wait_ge(nbest_ready, b)
                for t in range(TB):
                    last = act.activation(expl[:, t, :], logit[:, t, :], ACT.Exp, bias=nbest[:, t:t + 1])
                last.then_inc(expl_ready, 1)

            def step(region, b, g):
                one, two, three = (item(region, b, g, back) for back in range(1, LAG + 1))
                new = region != "tail"
                jobs = jobs_at(region, g)
                if g == 0 and region in ("first", "middle"):
                    take_ctx(b + 1)
                if g == 7 and region in ("middle", "last"):
                    weights_of(b)
                if new and g < G - 1:
                    evac_qk(b * G + g + 1, (g + 1) % 4)
                do(region, b, jobs[0])
                if one and qm_by_act(region, g):
                    evac_qm(*one)
                if two:
                    expo(*two, 0)
                    expo(*two, 1)
                do(region, b, jobs[1])
                if three:
                    evac_ot(*three)
                if new and g == G - 1 and region != "last":
                    evac_qk(b * G + G, 0)
                if new and g == 2:
                    copy_v(b)
                if two:
                    expo(*two, 2)
                    expo(*two, 3)
                do(region, b, jobs[2])

            act.wait_ge(ctx_in, 16)
            take_ctx(0)
            act.wait_ge(pads, 3)
            for name in prep:
                do("pro", -1, name)
            evac_qk(0, 0)

            def batch(region, b):
                for g in range(G):
                    step(region, b, g)

            regions(act, batch)
            for g in range(LAG):
                step("tail", B, g)
            do("tail", B, "attnT")
            do("tail", B, "ynT")
            weights_of(B)

            def silu(e, par):
                act.wait_ge(gu_full, e + 1)
                need(act, h_ready, e - 1)
                act.activation(sg[:, par, :], bank_gu[par][:, 0:I], ACT.Silu).then_inc(sg_ready, 1)

            def weigh(e, r, rounds):
                act.wait_ge(y_full, e + 1)
                need(act, acc_done[r % ACCS], 16 * ((RING // ACCS) * rounds + r // ACCS))
                act.activation(ye[:, r % ACCS, :], bank_y[r % 2][:, 0:D], ACT.Copy,
                               scale=xe[:, r, bass.ds(D + e, 1)]).then_inc(ye_ready, 1)

            silu(0, 0)
            silu(1, 1)
            for r in range(RING):
                silu(r + 2, r % 2)
                weigh(r, r, 0)
            with act.Fori(1, E // RING - 1) as it:
                for r in range(RING):
                    silu(it * RING + r + 2, r % 2)
                    weigh(it * RING + r, r, it)
            for r in range(RING):
                e = E - RING + r
                if e + 2 < E:
                    silu(e + 2, r % 2)
                weigh(e, r, E // RING - 1)

        @block.vector
        def _(dve):
            LT = Links(dve, table_links, 0)
            dve.wait_ge(small_in, 64)
            freqs = [10000.0 ** (-f / HALF) for f in range(HALF)]
            a4 = ang[:].rearrange("p t (a f) -> p t a f", f=HALF)
            for f in range(HALF):
                last = dve.tensor_scalar(a4[:, :, :, f], pos[:], freqs[f], None, ALU.mult)
            LT.link(last)
            LT.link(dve.tensor_scalar(turns[:], ang[:], 1.0 / TWO_PI, MAGIC, ALU.mult, ALU.add))
            LT.link(dve.tensor_scalar(turns[:], turns[:], MAGIC, None, ALU.subtract))
            hi, rest1 = two_part(TWO_PI)
            LT.link(dve.scalar_tensor_tensor(red[:], turns[:], -hi, ang[:], ALU.mult, ALU.add))
            LT.link(dve.scalar_tensor_tensor(red[:], turns[:], -rest1, red[:], ALU.mult, ALU.add))
            LT.link(dve.tensor_scalar(cosr[:], red[:], TWO_PI / 4, None, ALU.add))
            LT.link(dve.tensor_scalar(over[:], cosr[:], PI_F, -TWO_PI, ALU.is_gt, ALU.mult))
            LT.link(dve.tensor_tensor(cosr[:], cosr[:], over[:], ALU.add))
            LT.link(dve.tensor_scalar(cosr[:], cosr[:], PI_F, -PI_F, ALU.min, ALU.max))
            dve.tensor_scalar(red[:], red[:], PI_F, -PI_F, ALU.min, ALU.max).then_inc(tables, 1)
            dve.wait_ge(rw_T, 1)
            dve.tensor_copy(wrT[:].rearrange("p c e -> p (c e)"), psO[:, 0:DC * E]).then_inc(wrT_ready, 1)

            dve.wait_ge(x_in, 16)
            with dve.Fori(0, NT) as t:
                dve.bn_stats(stat1[:, bass.ds(t, 1), :].rearrange("p a s -> p (a s)"),
                             xall[:, bass.ds(t, 1), :].rearrange("p a d -> p (a d)")).then_inc(stat_links, 1)
            dve.wait_ge(stat_links, NT)
            for t in range(NT):
                last = dve.bn_aggr(mv1[:, t, :], stat1[:, t, :])
            last.then_inc(stats1, 1)
            dve.wait_ge(rstd1_ready, 1)

            def normalise(b, t):
                dve.tensor_scalar(xn[:, t, :], xall[:, bass.ds(b * TB + t, 1), :].rearrange("p a d -> p (a d)"),
                                  mv1[:, bass.ds(b * TB + t, 1), 0], rstd1[:, bass.ds(b * TB + t, 1)],
                                  ALU.subtract, ALU.mult).then_inc(xn_ready, 1)

            SPLIT_LINKS = 6

            def split(b, what, part):
                src, dst = (qsb, qsp) if what == "q" else (ksb, ksp)
                size = TB * H * PARTS
                to = dst[:, bass.ds((b % 2) * size, size)].rearrange("p (n r d) -> p n r d", r=PARTS // HD, d=HD)
                v = src[:].rearrange("p (n d) -> p n d", d=HD)
                r = rest[:].rearrange("p (n d) -> p n d", d=HD)
                n = TB * H

                def spread(ap, k):
                    return ap.unsqueeze(2).to_broadcast([P, n, k, HD])

                if part == 0:
                    dve.wait_ge(q_rot if what == "q" else k_rot, b + 1)
                    if what == "q":
                        dve.tensor_copy(to[:, :, PROD // HD, 0:2], zeros[:].unsqueeze(1).to_broadcast([P, n, 2]))
                        dve.tensor_copy(to[:, :, 0:3, :], spread(v, 3)).then_inc(split_links, 1)
                    else:
                        dve.tensor_copy(to[:, :, 4:6, :], spread(v, 2))
                        dve.tensor_copy(to[:, :, 0, :], v).then_inc(split_links, 1)
                    return
                if part == 1:
                    need(dve, split_done, 2 * b + (what == "k"))
                hold(dve, split_links, b * SPLIT_LINKS + (0 if what == "q" else 3) + part)
                if part == 1:
                    dve.tensor_tensor(r, v, to[:, :, 0, :], ALU.subtract).then_inc(split_links, 1)
                elif part == 2:
                    dve.tensor_copy(to[:, :, 3:5, :] if what == "q" else to[:, :, 1:4:2, :],
                                    spread(r, 2)).then_inc(split_links, 1)
                else:
                    dve.tensor_tensor(to[:, :, 5 if what == "q" else 2, :], r, to[:, :, 3, :],
                                      ALU.subtract).then_inc(split_done, 1)

            def row_max(b, g, j):
                dve.wait_ge(s_full, b * H + 4 * g + j + 1)
                if j == 0:
                    need(dve, m_ready, b * G + g - 1)
                dve.tensor_reduce(nmax[:, g % 2, :, j], psS[j % 2][:].rearrange("p (t k) -> p t k", t=TB), AX.X, ALU.max,
                                  negate=True).then_inc(max_done, 1)

            def store_max(b, g, part):
                size = TB * H * PARTS
                to = qsp[:, bass.ds((b % 2) * size, size)].rearrange("p (t h r) -> p t h r", t=TB, r=PARTS)
                to = to[:, :, 4 * g:4 * g + 4, :]
                if part == 0:
                    dve.wait_ge(max_done, b * H + 4 * g + 4)
                    dve.tensor_copy(to[:, :, :, PROD], nmax[:, g % 2]).then_inc(mhi_done, 1)
                else:
                    dve.wait_ge(mhi_done, b * G + g + 1)
                    dve.tensor_tensor(to[:, :, :, PROD + 1], nmax[:, g % 2], to[:, :, :, PROD],
                                      ALU.subtract).then_inc(m_ready, 1)

            def norm(b, g):
                o = ps_ot.rearrange("p (t j c) -> p t j c", t=TB, j=4)
                dve.wait_ge(ot_turned, b * G + g + 1)
                dve.reciprocal(rden[:], o[:, :, :, DEN]).then_inc(rden_done, 1)
                dve.wait_ge(rden_done, b * G + g + 1)
                dve.tensor_tensor(attn[:, :, g * 32:(g + 1) * 32].rearrange("p t (j d) -> p t j d", d=HD),
                                  o[:, :, :, 0:HD], rden[:].unsqueeze(3).to_broadcast([P, TB, 4, HD]),
                                  ALU.mult).then_inc(normed, 1)

            def evac_qm(b, g):
                dve.wait_ge(t2_full, b * G + g + 1)
                dve.tensor_copy(qm[:, g % 2, :], psT2[:, 0:2 * N]).then_inc(qm_ready, 1)

            LN_LINKS, ROUTE_LINKS = 2, 10

            def residual(region, b, part):
                n = use(region, b, "wout")
                mine = xall[:, bass.ds((b - 1) * TB, TB), :]
                if part == 0:
                    dve.wait_ge(biased, b)
                    dve.wait_ge(psx_full, n + 1)
                    dve.scalar_tensor_tensor(mine, psX[:].rearrange("p (t d) -> p t d", t=TB), gates[:, 2:3], mine,
                                             ALU.mult, ALU.add).then_inc(psx_free, 1)
                elif part == 1:
                    hold(dve, psx_free, n + 1)
                    for t in range(TB):
                        last = dve.bn_stats(stat2[:, t, :],
                                            xall[:, bass.ds((b - 1) * TB + t, 1), :].rearrange("p a d -> p (a d)"))
                    last.then_inc(ln_links, 1)
                elif part == 2:
                    hold(dve, ln_links, (b - 1) * LN_LINKS + 1)
                    for t in range(TB):
                        last = dve.bn_aggr(mv2[:, t, :], stat2[:, t, :])
                    last.then_inc(ln_links, 1)
                else:
                    dve.wait_ge(ln_links, (b - 1) * LN_LINKS + 2)
                    dve.tensor_scalar(mv2[:, :, 1], mv2[:, :, 1], 1e-5, None, ALU.add).then_inc(stats2, 1)

            def second_norm(b, t):
                dve.wait_ge(rstd2_ready, b)
                need(dve, scattered, 16 * NSC * (b - 1))
                dve.tensor_scalar(rows[:, t, 0:D], xall[:, bass.ds((b - 1) * TB + t, 1), :].rearrange("p a d -> p (a d)"),
                                  mv2[:, t, 0:1], rstd2[:, t:t + 1], ALU.subtract, ALU.mult).then_inc(y_ready, 1)

            def choose(region, b, part):
                n = use(region, b, "logit")
                links = (b - 1) * ROUTE_LINKS
                if part == 0:
                    dve.wait_ge(psx_full, n + 1)
                    dve.tensor_copy(logit[:].rearrange("p t e -> p (t e)"), psX[:, 0:TB * E]).then_inc(psx_free, 1)
                elif part == 1:
                    hold(dve, psx_free, n + 1)
                    for t in range(TB):
                        last = dve.max(best[:, t, :], logit[:, t, :])
                    last.then_inc(route_links, 1)
                elif part == 2:
                    dve.wait_ge(route_links, links + 1)
                    dve.tensor_scalar(nbest[:], best[:, :, 0], -1.0, None, ALU.mult).then_inc(nbest_ready, 1)
                    for t in range(TB):
                        last = dve.match_replace(cut[:, t, :], best[:, t, :], logit[:, t, :], -3.0e38)
                    last.then_inc(route_links, 1)
                elif part == 3:
                    dve.wait_ge(route_links, links + 2)
                    dve.tensor_tensor(chosen[:], cut[:], logit[:], ALU.not_equal).then_inc(route_links, 1)
                else:
                    dve.wait_ge(route_links, links + 3)
                    dve.tensor_copy(chosenb[:], chosen[:]).then_inc(chosen_ready, 1)

            def weigh_choice(b, part):
                links = (b - 1) * ROUTE_LINKS
                if part == 0:
                    dve.wait_ge(expl_ready, b)
                    dve.tensor_tensor(wbuf[:], expl[:], chosen[:], ALU.mult).then_inc(route_links, 1)
                elif part == 1:
                    dve.wait_ge(route_links, links + 4)
                    dve.tensor_reduce(wsum[:], wbuf[:], AX.X, ALU.add).then_inc(route_links, 1)
                elif part == 2:
                    dve.wait_ge(route_links, links + 5)
                    dve.reciprocal(wrec[:], wsum[:]).then_inc(route_links, 1)
                else:
                    dve.wait_ge(route_links, links + 6)
                    dve.tensor_tensor(rows[:, :, D:ID], wbuf[:], wrec[:].unsqueeze(2).to_broadcast([P, TB, E]), ALU.mult)

            def place_choice(region, b):
                n = use(region, b, "rank")
                links = (b - 1) * ROUTE_LINKS
                dve.wait_ge(psx_full, n + 1)
                rank = psX[:, 0:TB * E].rearrange("p (t e) -> p t e", t=TB)
                dve.tensor_scalar(drop[:], rank, float(C), 2.0 * E * C, ALU.is_ge, ALU.mult)
                dve.tensor_tensor(place[:], rank, slot0[:].rearrange("p (t e) -> p t e", t=TB), ALU.add).then_inc(route_links, 1)
                dve.wait_ge(route_links, links + 7)
                dve.tensor_tensor(place[:], place[:], drop[:], ALU.max).then_inc(psx_free, 1)
                dve.wait_ge(psx_free, n + 1)
                dve.scalar_tensor_tensor(place[:], place[:], 1.0, chosen[:], ALU.add, ALU.mult).then_inc(route_links, 1)
                hold(dve, route_links, links + 8)
                for t in range(TB):
                    last = dve.max(best8[:, t, :], place[:, t, :])
                last.then_inc(route_links, 1)
                dve.tensor_tensor(seen[:], seen[:], chosenb[:, 0, :], ALU.add).then_inc(route_links, 1)
                dve.wait_ge(route_links, links + 9)
                dve.tensor_scalar(idx[:], best8[:], 1.0, None, ALU.subtract).then_inc(idx_ready, 1)
                dve.wait_ge(route_links, links + 10)
                dve.tensor_tensor(seen[:], seen[:], chosenb[:, 1, :], ALU.add).then_inc(seen_done, 1)

            BESIDE = {0: (["n0"], [], ["n1"], [], []),
                      4: (["q0"], ["r0"], ["r1"], ["r2"], ["r3"]),
                      5: (["y0"], ["y1"], ["q1"], ["q2"], ["q3"]),
                      6: (["k0"], ["c0"], ["c1", "k1"], ["c2"], ["c3", "c4"]),
                      7: (["k2", "w0"], ["k3", "w1"], ["w2"], ["w3"], [])}

            def beside(region, b, g, where):
                for name in BESIDE.get(g, [[]] * 5)[where]:
                    kind, part = name[0], int(name[1])
                    if region in ("first", "middle"):
                        if kind == "n":
                            normalise(b + 1, part)
                        elif kind in "qk":
                            split(b + 1, kind, part)
                    if region in ("middle", "last"):
                        if kind == "r":
                            residual(region, b, part)
                        elif kind == "y":
                            second_norm(b, part)
                        elif kind == "c":
                            choose(region, b, part)
                        elif kind == "w":
                            weigh_choice(b, part)

            def step(region, b, g):
                one, three = item(region, b, g, 1), item(region, b, g, LAG)
                new = region != "tail"
                if new:
                    row_max(b, g, 0)
                beside(region, b, g, 0)
                if new:
                    row_max(b, g, 1)
                if one and not qm_by_act(region, g):
                    evac_qm(*one)
                beside(region, b, g, 1)
                if new:
                    row_max(b, g, 2)
                beside(region, b, g, 2)
                if new:
                    row_max(b, g, 3)
                if new:
                    store_max(b, g, 0)
                beside(region, b, g, 3)
                if new:
                    store_max(b, g, 1)
                beside(region, b, g, 4)
                if g == 7 and region in ("middle", "last"):
                    place_choice(region, b)
                if g == LAG and region in ("middle", "last"):
                    dve.wait_ge(psx_full, use(region, b, "attnT") + 1)
                if three:
                    norm(*three)

            for t in range(TB):
                normalise(0, t)
            dve.wait_ge(gates_ready, 1)
            dve.wait_ge(pads, 3)
            for what in ("q", "k"):
                for part in range(4):
                    split(0, what, part)

            def batch(region, b):
                for g in range(G):
                    step(region, b, g)

            regions(dve, batch)
            for g in range(LAG):
                step("tail", B, g)
            for part in range(4):
                residual("tail", B, part)
            for t in range(TB):
                second_norm(B, t)
            for part in range(5):
                choose("tail", B, part)
            for part in range(4):
                weigh_choice(B, part)
            place_choice("tail", B)

            def evac_xT(e, par):
                dve.wait_ge(xeT_full, e + 1)
                need(dve, gu_full, e - 1)
                dve.tensor_copy(xeT[:, par, :], bank_xT[par][:, 0:DC * C]).then_inc(xeT_ready, 1)

            def times_up(e, par):
                dve.wait_ge(sg_ready, e + 1)
                need(dve, hT_full, e - 1)
                dve.tensor_tensor(hsb[:, par, :], bank_gu[par][:, I:I2], sg[:, par, :], ALU.mult).then_inc(h_ready, 1)

            def evac_hT(e, par):
                dve.wait_ge(hT_full, e + 1)
                need(dve, y_full, e - 1)
                dve.tensor_copy(hT[0:I, par, :], bank_hT[par][0:I, 0:C]).then_inc(hT_ready, 1)

            def estep(s, k):
                known = isinstance(s, int)
                if not (known and s + 2 >= E):
                    evac_xT(s + 2, k % 2)
                if not (known and (s + 1 < 0 or s + 1 >= E)):
                    times_up(s + 1, (k + 1) % 2)
                if not (known and (s < 0 or s >= E)):
                    evac_hT(s, k % 2)

            for s in range(-2, 3):
                estep(s, s)
            LOOPS = (E - 5) // RING
            with dve.Fori(0, LOOPS) as it:
                for k in range(3, RING + 3):
                    estep(it * RING + k, k)
            for s in range(LOOPS * RING + 3, E + 1):
                estep(s, s)

            L = Links(dve, fin_links, 0)
            for a in range(ACCS):
                dve.wait_ge(fin_in[a], 32)
                for h in range(2):
                    mine = xall[:, 4 * h:4 * h + 4, :]
                    last = dve.scalar_tensor_tensor(mine, fin[a][:, 4 * h:4 * h + 4, :], gates[:, 3:4], mine,
                                                    ALU.mult, ALU.add)
                    if a == ACCS - 1:
                        last.then_inc(out_ready, 1)
                if a < ACCS - 1:
                    L.link(last)

        @block.gpsimd
        def _(pool):
            pool.memset(zrow[:], 0.0).then_inc(pool_links, 1)
            pool.wait_ge(pool_links, 1)
            pool.iota(zrow[:, ID:ID + 1].bitcast(I32), [[0, 1]], base=T, channel_multiplier=1).then_inc(zrow_ready, 1)
            pool.memset(identf[:], 0.0).then_inc(pool_links, 1)
            pool.memset(before[:], 0.0).then_inc(pool_links, 1)
            pool.wait_ge(pool_links, 3)
            pool.affine_select(out=identf[:], in_=identf[:], compare_op=ALU.not_equal, fill=1.0, base=0,
                               pattern=[[-1, P]], channel_multiplier=1).then_inc(pool_links, 1)
            pool.affine_select(out=before[:], in_=before[:], compare_op=ALU.is_ge, fill=1.0, base=0,
                               pattern=[[-1, P]], channel_multiplier=1)
            pool.memset(onesb[:], 1.0)
            pool.memset(seen[:], 0.0)
            pool.memset(zeros[:], 0.0)
            pool.memset(half_neg[:], -0.5)
            pool.wait_ge(pool_links, 4)
            pool.tensor_copy(identb[:], identf[:]).then_inc(consts, 1)
            q16 = qsp[:].rearrange("p (n r) -> p n r", r=PARTS)
            k16 = ksp[:].rearrange("p (n r) -> p n r", r=PARTS)
            pool.memset(q16[:, :, PROD:PARTS].bitcast(F32), 0.0).then_inc(pads, 1)
            pool.memset(k16[:, :, MAXROWS:PARTS].bitcast(F32), 0.0)
            pool.memset(k16[:, :, PROD:MAXROWS], 1.0).then_inc(pads, 1)
            pool.memset(vaug[:], 0.0).then_inc(pool_links, 1)
            pool.wait_ge(pool_links, 5)
            pool.memset(vaug[:].rearrange("p t (h c) -> p (t h) c", c=VCOLS)[:, :, DEN:DEN + 1], 1.0).then_inc(pads, 1)
            pool.iota(ids[:], [[P, NT]], base=0, channel_multiplier=1)
            pool.iota(slot_i[:], [[0, TB], [C, E]], base=0, channel_multiplier=0).then_inc(pool_links, 1)
            pool.wait_ge(pool_links, 6)
            pool.tensor_copy(slot0[:], slot_i[:]).then_inc(pool_links, 1)
            pool.memset(rows[:, :, ID:ROW], 0.0).then_inc(rows_ready, 1)

            pool.wait_ge(stats1, 1)
            pool.tensor_scalar(rstd1[:], mv1[:, :, 1], 1e-5, None, ALU.add).then_inc(pool_links, 1)
            pool.wait_ge(pool_links, 8)
            pool.tensor_tensor(rstd1[:], rstd1[:], half_neg[:], ALU.pow).then_inc(rstd1_ready, 1)
            pool.wait_ge(sin_done, 1)

            def rotate(region, b, what):
                buf, done = (qsb, q_rot) if what == "q" else (ksb, k_rot)
                if what == "k":
                    pool.wait_ge(q_rot, b + 2)
                else:
                    need(pool, k_rot, b + 1)
                hold(pool, psx_free, use(region, b, "q" if what == "q" else "kv1") + 1)
                if what == "q":
                    hold(pool, split_done, 2 * b + 2)
                L = Links(pool, rope_links, (b + 1) * 2 + (0 if what == "q" else 1))
                n = [P, TB, H, HD]
                v = buf[:].rearrange("p (t h d) -> p t h d", t=TB, d=HD)
                a = rt[:].rearrange("p (t h d) -> p t h d", t=TB, d=HD)
                c = cosT[:, bass.ds((b + 1) * TB, TB), :].unsqueeze(2).to_broadcast(n)
                v2 = buf[:].rearrange("p (t h f a) -> p t (h f) a", t=TB, h=H, a=2)
                r2 = rt2[:].rearrange("p (t h f a) -> p t (h f) a", t=TB, h=H, a=2)
                pool.tensor_tensor(a, v, c, ALU.mult)
                for o in range(2):
                    s = sinT[:, bass.ds((b + 1) * TB, TB), o::2].unsqueeze(2).to_broadcast([P, TB, H, HD // 2])
                    vo = buf[:].rearrange("p (t h f a) -> p t h f a", t=TB, h=H, a=2)[:, :, :, :, 1 - o]
                    ro = rt2[:].rearrange("p (t h f a) -> p t h f a", t=TB, h=H, a=2)[:, :, :, :, o]
                    last = pool.tensor_tensor(ro, vo, s, ALU.mult)
                L.link(last)
                pool.tensor_tensor(buf[:], rt[:], rt2[:], ALU.add).then_inc(done, 1)

            def root(b):
                pool.wait_ge(stats2, b)
                pool.tensor_tensor(rstd2[:], mv2[:, :, 1], half_neg[:, 0:TB], ALU.pow).then_inc(rstd2_ready, 1)

            def scatter(b):
                need(pool, scattered, 16 * NSC * (b - 1))
                hold(pool, rows_ready, b)
                pool.tensor_copy(rows[:, :, ID].bitcast(I32), ids[:, bass.ds((b - 1) * TB, TB)]).then_inc(rows_ready, 1)
                pool.wait_ge(rows_ready, b + 1)
                hold(pool, idx_ready, b)
                for t in range(TB):
                    for k in range(TOPK):
                        pool.indirect_dma_start(out=slots, out_offset=bass.IndirectOffsetOnAxis(ap=idx[:, t, k:k + 1], axis=0),
                                                in_=rows[:, t, :], in_offset=None, bounds_check=E * C - 1,
                                                oob_is_err=False).then_inc(scattered, 16)

            def bias(b):
                hold(pool, xn_ready, TB * (b + 1))
                mine = xall[:, bass.ds(b * TB, TB), :]
                pool.tensor_tensor(mine, mine, boutg[:].unsqueeze(1).to_broadcast([P, TB, D]), ALU.add).then_inc(biased, 1)

            rotate("pro", -1, "q")
            rotate("pro", -1, "k")
            pool.wait_ge(gates_ready, 1)
            pool.wait_ge(wproj_in, 64)
            pool.tensor_scalar(boutg[:], boutg[:], gates[:, 2:3], None, ALU.mult).then_inc(pool_links, 1)
            pool.wait_ge(pool_links, 9)
            bias(0)

            def batch(region, b):
                if region != "last":
                    rotate(region, b, "q")
                    rotate(region, b, "k")
                    bias(b + 1)
                if region != "first":
                    root(b)
                    scatter(b)
                else:
                    pool.wait_ge(slots_filled, 16)

            regions(pool, batch)
            root(B)
            scatter(B)

            def add_rows(e, r, rounds):
                pool.wait_ge(ye_ready, e + 1)
                hold(pool, acc_done[r % ACCS], 16 * ((RING // ACCS) * rounds + r // ACCS))
                pool.indirect_dma_start(out=acc[r % ACCS],
                                        out_offset=bass.IndirectOffsetOnAxis(ap=xe[:, r, ID:ID + 1].bitcast(U32), axis=0),
                                        in_=ye[:, r % ACCS, :], in_offset=None, bounds_check=T + P - 1, oob_is_err=True,
                                        compute_op=ALU.add).then_inc(acc_done[r % ACCS], 16)

            pool.wait_ge(acc_filled, 16 * ACCS)
            with pool.Fori(0, E // RING) as it:
                for r in range(RING):
                    add_rows(it * RING + r, r, it)


_INS = ["x", "ctx_1024", "fside_BxSx2_0", "g_xattn", "g_ffn", "L0_xattn_Wq", "L0_xattn_Wkv", "L0_xattn_Wout",
        "L0_xattn_bout", "L0_ffn_router_weight", "L0_ffn_gate_up_proj", "L0_ffn_down_proj"]


def kernel(**inputs):
    import numpy as _np
    import concourse.bacc as _bacc
    from concourse import mybir as _mybir
    from concourse.bass_utils import run_bass_kernel_spmd as _run

    nc = _bacc.Bacc("TRN2", target_bir_lowering=False, num_devices=1)
    arrays, args = {}, []
    for name in _INS:
        a = _np.ascontiguousarray(inputs[name])
        arrays[f"in_{name}"] = a
        args.append(nc.dram_tensor(f"in_{name}", a.shape, _mybir.dt.from_np(a.dtype), kind="ExternalInput").ap())
    shape = inputs["x"].shape
    out = nc.dram_tensor("out_0", shape, _mybir.dt.float32, kind="ExternalOutput").ap()
    flamingo(nc, *args, out)
    r = _run(nc, [arrays], core_ids=[0])
    return r.results[0]["out_0"]
```

```python
from contextlib import ExitStack

import concourse.bass as bass
from concourse import mybir

P = 128
F32 = mybir.dt.float32
BF16 = mybir.dt.bfloat16
U32 = mybir.dt.uint32
I32 = mybir.dt.int32
ALU = mybir.AluOpType
ACT = mybir.ActivationFunctionType
AX = mybir.AxisListType

PARTS = 64
PROD = 48
MAXROWS = 50
VCOLS = 32
LAG = 3
DEN = 8
ACCS = 4
FINAL = 7
RING = 16
CHUNK = 2
TOPK = 8
TWO_PI = 6.283185307179586
PI_F = 3.1415925
MAGIC = 12582912.0


def need(eng, sem, value):
    if isinstance(value, int) and value <= 0:
        return
    eng.wait_ge(sem, value)


def hold(eng, sem, value):
    eng.wait_ge(sem, value)
    eng.nop(nofuse=True)


class Links:

    def __init__(self, eng, sem, base):
        self.eng, self.sem, self.base, self.n = eng, sem, base, 0

    def link(self, ins):
        self.n += 1
        ins.then_inc(self.sem, 1)
        hold(self.eng, self.sem, self.base + self.n)


def two_part(v):
    hi = float(int(v * 256)) / 256
    return hi, v - hi


def flamingo(nc, x, ctx_1024, fside_BxSx2_0, g_xattn, g_ffn, L0_xattn_Wq, L0_xattn_Wkv, L0_xattn_Wout,
             L0_xattn_bout, L0_ffn_router_weight, L0_ffn_gate_up_proj, L0_ffn_down_proj, out):
    B, N, D = x.shape
    CD = ctx_1024.shape[2]
    HD = 8
    H = D // HD
    T = B * N
    NT = T // P
    TB = N // P
    G = H // 4
    E, _, I2 = L0_ffn_gate_up_proj.shape
    I = I2 // 2
    C = P
    DC = D // P
    ROW = D + E + 4
    ID = D + E
    ITEMS = B * G
    SCALE = float(HD) ** -0.5
    NSC = TB * TOPK
    HALF = HD // 4
    LATE = E // 4
    ROUND_IN = 16 * RING // CHUNK
    assert LATE == RING and E == 4 * RING
    assert (N, D, CD, H, E, I, TB, G, DC, HALF) == (256, 256, 128, 32, 64, 96, 2, 8, 2, 2)

    xf = x.rearrange("b n d -> (b n) d").rearrange("(t p) d -> p t d", p=P)
    of = out.rearrange("b n d -> (b n) d").rearrange("(t p) d -> p t d", p=P)
    ctxf = ctx_1024.rearrange("b n d -> (b n) d").rearrange("(t p) d -> p t d", p=P)
    posf = fside_BxSx2_0.rearrange("b n d -> (b n) d").rearrange("(t p) d -> p t d", p=P)
    wgu_src = L0_ffn_gate_up_proj.rearrange("e (p c) f -> p e (c f)", c=DC)
    wd_src = L0_ffn_down_proj.rearrange("e i h -> i e h")

    slots = nc.dram_tensor("slots", [E * C, ROW], F32, kind="Internal").ap()
    acc = [nc.dram_tensor(f"acc{a}", [T + P, D], F32, kind="Internal").ap() for a in range(ACCS)]

    with ExitStack() as ctx:
        arena = (nc.sbuf_base + 63) // 64 * 64
        top = [arena]

        def at(name, shape, dt, offset):
            return nc.alloc_sbuf_tensor_at(name, shape, dt, offset=offset)

        def sb(name, shape, dt):
            n = 4 if dt != BF16 else 2
            for s in shape[1:]:
                n *= s
            here = top[0]
            top[0] = (here + n + 31) // 32 * 32
            return at(name, shape, dt, here)

        def sem(name):
            return ctx.enter_context(nc.semaphore(name))

        def psum(name, shape, dt):
            return ctx.enter_context(nc.psum_tensor(name, shape, dt))

        wd = sb("wd", [P, E, D], F32)
        gu_base = top[0]
        wgu = sb("wgu", [P, E, DC * I2], F32)
        late = gu_base + LATE * DC * I2 * 4
        end_of_weights = top[0]
        top[0] = late
        qsp = sb("qsp", [P, 2 * TB * H * PARTS], BF16)
        ksp = sb("ksp", [P, 2 * TB * H * PARTS], BF16)
        probs = sb("probs", [P, 2, 4 * 2 * N], F32)
        vaug = sb("vaug", [P, TB, H * VCOLS], F32)
        qT = sb("qT", [P, 4, 2 * N], BF16)
        kT = sb("kT", [P, 4, 2, 2 * N], BF16)
        qm = sb("qm", [P, 2, 2 * N], BF16)
        ksb = sb("ksb", [P, TB * D], F32)
        assert top[0] <= end_of_weights, (top[0], end_of_weights)
        top[0] = end_of_weights
        xall = sb("xall", [P, NT, D], F32)
        identf = sb("identf", [P, P], F32)
        identb = sb("identb", [P, P], BF16)
        before = sb("before", [P, P], BF16)
        onesb = sb("onesb", [P, P], BF16)
        boutg = sb("boutg", [P, D], F32)
        slot0 = sb("slot0", [P, TB * E], F32)
        slot_i = sb("slot_i", [P, TB * E], I32)
        ids = sb("ids", [P, NT], I32)
        half_neg = sb("half_neg", [P, NT], F32)
        gates = sb("gates", [P, 4], F32)
        wrT = sb("wrT", [P, DC, E], F32)
        stat2 = sb("stat2", [P, TB, 6], F32)
        mv2 = sb("mv2", [P, TB, 2], F32)
        rstd2 = sb("rstd2", [P, TB], F32)
        wbuf = sb("wbuf", [P, TB, E], F32)
        rows = sb("rows", [P, TB, ROW], F32)
        idx = sb("idx", [P, TB, TOPK], U32)
        logit = sb("logit", [P, TB, E], F32)
        best = sb("best", [P, TB, 8], F32)
        nbest = sb("nbest", [P, TB], F32)
        cut = sb("cut", [P, TB, E], F32)
        chosen = sb("chosen", [P, TB, E], F32)
        chosenb = sb("chosenb", [P, TB, E], BF16)
        zeros = sb("zeros", [P, 2], BF16)
        seen = sb("seen", [P, E], BF16)
        expl = sb("expl", [P, TB, E], F32)
        wrec = sb("wrec", [P, TB], F32)
        exp8 = sb("exp8", [P, TB, 8], F32)
        wsum = sb("wsum", [P, TB], F32)
        place = sb("place", [P, TB, E], F32)
        drop = sb("drop", [P, TB, E], F32)
        best8 = sb("best8", [P, TB, TOPK], F32)
        shared = top[0]
        qsb = sb("qsb", [P, TB * D], F32)
        rt = sb("rt", [P, TB * D], F32)
        vstage = sb("vstage", [P, TB, D], F32)
        rt2 = sb("rt2", [P, TB * D], F32)
        rest = sb("rest", [P, TB * D], F32)
        xn = sb("xn", [P, TB, D], F32)
        ctxc = sb("ctxc", [P, TB, CD], F32)
        ctxT = sb("ctxT", [P, N], F32)
        wq_at = top[0]
        wq = sb("wq", [P, DC * D], F32)
        wkv = sb("wkv", [P, 2 * D], F32)
        wq_end = top[0]
        otsb = sb("otsb", [P, 2, N], F32)
        attn = sb("attn", [P, TB, D], F32)
        attnT = sb("attnT", [P, DC, N], F32)
        xT = sb("xT", [P, DC, N], F32)
        wout = sb("wout", [P, DC * D], F32)
        pos = sb("pos", [P, NT, 2], F32)
        cosT = sb("cosT", [P, NT, HD], F32)
        sinT = sb("sinT", [P, NT, HD], F32)
        nmax = sb("nmax", [P, 2, TB, 4], F32)
        rden = sb("rden", [P, TB, 4], F32)
        stat1 = sb("stat1", [P, NT, 6], F32)
        mv1 = sb("mv1", [P, NT, 2], F32)
        rstd1 = sb("rstd1", [P, NT], F32)
        assert 4 * TB * ROW <= wq_end - wq_at
        rows_last = at("rows_last", [P, TB, ROW], F32, wq_at)
        end_attn = top[0]
        assert end_attn <= nc.sbuf_usable_end, (end_attn, nc.sbuf_usable_end)
        top[0] = shared
        xe = sb("xe", [P, RING, ROW], F32)
        ye = sb("ye", [P, ACCS, D], F32)
        xeT = sb("xeT", [P, 2, DC * C], F32)
        hsb = sb("hsb", [P, 2, I], F32)
        sg = sb("sg", [P, 2, I], F32)
        hT = sb("hT", [P, 2, C], F32)
        assert top[0] <= nc.sbuf_usable_end
        fin = [at(f"fin{a}", [P, NT, D], F32, arena + a * NT * D * 4) for a in range(ACCS)]
        ctxall = at("ctxall", [P, NT, CD], F32, late - 4 * NT * CD)
        rw = at("rw", [E, D], F32, late - 4 * NT * CD - 4 * D)
        ang_at = late - 4 * NT * CD - 4 * D - 6 * NT * 4 * 4
        ang, turns, red, cosr, over = (at(f"angle{i}", [P, NT, 4], F32, ang_at + i * NT * 4 * 4) for i in range(5))
        zrow = at("zrow", [P, ROW], F32, (ang_at - 4 * ROW) // 32 * 32)
        early = LATE - 8

        psT1 = psum("psT1", [P, 4 * N], BF16)
        psT2 = psum("psT2", [P, 4 * N], BF16)
        psS = [psum(f"psS{i}", [P, 2 * N], F32) for i in range(2)]
        psST = [psum(f"psST{i}", [P, 2 * N], F32) for i in range(2)]
        psO = psum("psO", [P, 2 * N], F32)
        psX = psum("psX", [P, 2 * N], F32)
        ps_ot = psO[:, N:2 * N]
        bank_xT = [psS[0], psS[1]]
        bank_gu = [psST[0], psST[1]]
        bank_hT = [psO, psX]
        bank_y = [psT1[:, :].bitcast(F32), psT2[:, :].bitcast(F32)]

        x_in, x_rest_in, ctx_in, ctx_rest_in = sem("x_in"), sem("x_rest_in"), sem("ctx_in"), sem("ctx_rest_in")
        pos_in, small_in = sem("pos_in"), sem("small_in")
        wkv_in, wq_in, wout_in = sem("wkv_in"), sem("wq_in"), sem("wout_in")
        wd_in = [sem(f"wd_in{i}") for i in range(4)]
        wgu_in = [sem(f"wgu_in{i}") for i in range(LATE // 8)]
        wgu_late = sem("wgu_late")
        acc_done = [sem(f"acc_done{a}") for a in range(ACCS)]
        slots_filled, acc_filled = sem("slots_filled"), sem("acc_filled")
        consts, zrow_ready = sem("consts"), sem("zrow_ready")
        table_links, sin_done, tables = sem("table_links"), sem("sin_done"), sem("tables")
        rw_T, wrT_ready = sem("rw_T"), sem("wrT_ready")
        stats1, rstd1_ready, gates_ready = sem("stats1"), sem("rstd1_ready"), sem("gates_ready")
        stat_links = sem("stat_links")
        xn_ready, ctxc_ready = sem("xn_ready"), sem("ctxc_ready")
        psx_full, psx_free = sem("psx_full"), sem("psx_free")
        v_staged = sem("v_staged")
        q_rot, k_rot, rope_links = sem("q_rot"), sem("k_rot"), sem("rope_links")
        turn_links = sem("turn_links")
        q_split_links, q_split = sem("q_split_links"), sem("q_split")
        k_hi, k_rest, k_mid, k_split = sem("k_hi"), sem("k_rest"), sem("k_mid"), sem("k_split")
        pads = sem("pads")
        t1_full, qk_ready = sem("t1_full"), sem("qk_ready")
        s_full, max_done, mhi_done, m_ready = sem("s_full"), sem("max_done"), sem("mhi_done"), sem("m_ready")
        t2_full, qm_ready = sem("t2_full"), sem("qm_ready")
        st_full, exp_done, pv_done = sem("st_full"), sem("exp_done"), sem("pv_done")
        ot_ready, rden_done, v_ready = sem("ot_ready"), sem("rden_done"), sem("v_ready")
        ot_turned, normed, biased = sem("ot_turned"), sem("normed"), sem("biased")
        stats2, rstd2_ready, y_ready = sem("stats2"), sem("rstd2_ready"), sem("y_ready")
        ln_links, route_links = sem("ln_links"), sem("route_links")
        nbest_ready, expl_ready, chosen_ready, idx_ready = (
            sem("nbest_ready"), sem("expl_ready"), sem("chosen_ready"), sem("idx_ready"))
        wrec_ready = sem("wrec_ready")
        weigh_links, weighed, seen_done = sem("weigh_links"), sem("weighed"), sem("seen_done")
        rows_ready = sem("rows_ready")
        scattered = sem("scattered")
        xe_in = [sem(f"xe_in{i}") for i in range(RING)]
        xeT_full, xeT_ready, gu_full, sg_ready, h_ready = (
            sem("xeT_full"), sem("xeT_ready"), sem("gu_full"), sem("sg_ready"), sem("h_ready"))
        hT_full, hT_ready, y_full, ye_ready = sem("hT_full"), sem("hT_ready"), sem("y_full"), sem("ye_ready")
        fin_in = [sem(f"fin_in{n}") for n in range(ACCS - 1)]
        fin_last_in = [sem(f"fin_last_in{b}") for b in range(B)]
        pool_links = sem("pool_links")
        fin_links, out_ready, out_done = sem("fin_links"), sem("out_ready"), sem("out_done")

        prep = ["ctxT", "xnT", "q", "kv0", "kv1"]
        SLOT = {0: ("ctxT", None, "xnT"), 1: ("q_a", None, "q"), 2: (None, None, "kv0"), 3: ("kv1", "attnT", "wout_a"),
                4: ("wout", None, None), 5: (None, "ynT", "logit"), 7: ("rank", None, None)}
        epi = ["attnT", "wout", "ynT", "logit", "rank"]

        def jobs_of(names, slot):
            return [name for g in range(G) for name in slot.get(g, ()) if name in names]

        FIRST, MIDDLE, LAST, TAIL = jobs_of(prep, SLOT), jobs_of(prep + epi, SLOT), jobs_of(epi, SLOT), epi
        BASE1 = len(prep) + len(FIRST)
        BASE_LAST = BASE1 + (B - 2) * len(MIDDLE)
        BASE_TAIL = BASE_LAST + len(LAST)

        def use(region, b, name):
            if region == "pro":
                return ["ctxT", "kv0", "kv1", "xnT", "q"].index(name)
            if region == "first":
                return len(prep) + FIRST.index(name)
            if region == "middle":
                return BASE1 + (b - 1) * len(MIDDLE) + MIDDLE.index(name)
            if region == "last":
                return BASE_LAST + LAST.index(name)
            return BASE_TAIL + TAIL.index(name)

        def jobs_at(region, g):
            has = {"first": prep, "middle": prep + epi, "last": epi, "tail": []}[region]
            return [n if n and n.removesuffix("_a") in has else None for n in SLOT.get(g, (None,) * 3)]

        def item(region, b, g, back):
            if region == "tail" and g >= back:
                return None
            if g >= back:
                return b, g - back
            return None if region == "first" else (b - 1, g - back + G)

        def regions(eng, body):
            body("first", 0)
            with eng.Fori(1, B - 1) as b:
                body("middle", b)
            body("last", B - 1)

        K_COPIES = {4: "hi", 5: "mid"}

        def rows_of(region):
            return rows_last if region == "tail" else rows

        def qm_by_act(region, g):
            return g in (4, 5, 7) and region != "tail"

        def turn(eng, b, what, one, other, links, n):
            buf, done = (qsb, q_rot) if what == "q" else (ksb, k_rot)
            v = buf[:].rearrange("p (t h d) -> p t h d", t=TB, d=HD)
            pairs = buf[:].rearrange("p (t h f a) -> p t h f a", t=TB, h=H, a=2)
            crossed = other.rearrange("p (t h f a) -> p t h f a", t=TB, h=H, a=2)
            c = cosT[:, bass.ds(b * TB, TB), :].unsqueeze(2).to_broadcast([P, TB, H, HD])
            eng.tensor_tensor(one.rearrange("p (t h d) -> p t h d", t=TB, d=HD), v, c, ALU.mult)
            for o in range(2):
                s = sinT[:, bass.ds(b * TB, TB), o::2].unsqueeze(2).to_broadcast([P, TB, H, HD // 2])
                last = eng.tensor_tensor(crossed[:, :, :, :, o], pairs[:, :, :, :, 1 - o], s, ALU.mult)
            last.then_inc(links, 1)
            hold(eng, links, n)
            eng.tensor_tensor(buf[:], one, other, ALU.add).then_inc(done, 1)

        def acc_of(e):
            return e % ACCS if e < E - FINAL else 1 + (e - E + FINAL) % (ACCS - 1)

        def additions(a, e):
            return sum(acc_of(x) == a for x in range(e))

        by_end = sorted(range(ACCS), key=lambda a: max(e for e in range(E) if acc_of(e) == a))

        def parts_of(buf, b):
            size = TB * H * PARTS
            return buf[:, bass.ds((b % 2) * size, size)].rearrange("p (n r d) -> p n r d", r=PARTS // HD, d=HD)

        def by_head(buf):
            return buf[:].rearrange("p (n d) -> p n d", d=HD)

        def spread(ap, k):
            return ap.unsqueeze(2).to_broadcast([P, TB * H, k, HD])

        block = ctx.enter_context(nc.Block())

        @block.sync
        def _(sp):
            sp.dma_start(xall[:, 0:TB, :], xf[:, 0:TB, :]).then_inc(x_in, 16)
            sp.dma_start(ctxall[:, 0:TB, :], ctxf[:, 0:TB, :]).then_inc(ctx_in, 16)
            sp.dma_start(pos[:], posf).then_inc(pos_in, 16)
            sp.dma_start(wkv[:], L0_xattn_Wkv).then_inc(wkv_in, 16)
            sp.dma_start(wq[:], L0_xattn_Wq.rearrange("(p c) n -> p (c n)", c=DC)).then_inc(wq_in, 16)
            sp.dma_start(xall[:, TB:NT, :], xf[:, TB:NT, :]).then_inc(x_rest_in, 16)
            sp.dma_start(ctxall[:, TB:NT, :], ctxf[:, TB:NT, :]).then_inc(ctx_rest_in, 16)
            sp.dma_start(rw[:], L0_ffn_router_weight).then_inc(small_in, 16)
            sp.dma_start(gates[:, 0:1], g_xattn.partition_broadcast(P)).then_inc(small_in, 16)
            sp.dma_start(gates[:, 1:2], g_ffn.partition_broadcast(P)).then_inc(small_in, 16)
            sp.dma_start(boutg[:], L0_xattn_bout.partition_broadcast(P)).then_inc(small_in, 16)
            sp.dma_start(wout[:], L0_xattn_Wout.rearrange("(p c) n -> p (c n)", c=DC)).then_inc(wout_in, 16)
            sp.wait_ge(zrow_ready, 1)
            sp.dma_start(slots.rearrange("(e c) r -> c e r", c=C),
                         zrow[:].unsqueeze(1).to_broadcast([P, E, ROW])).then_inc(slots_filled, 16)
            for i in range(4):
                n = E // 4
                sp.dma_start(wd[0:I, i * n:(i + 1) * n, :], wd_src[:, i * n:(i + 1) * n, :]).then_inc(wd_in[i], 16)
            for a in range(ACCS):
                sp.dma_start(acc[a].rearrange("(t p) d -> p t d", p=P),
                             zrow[:, 0:D].unsqueeze(1).to_broadcast([P, NT + 1, D])).then_inc(acc_filled, 16)

            def load_gu(i):
                sp.dma_start(wgu[:, 8 * i:8 * i + 8, :], wgu_src[:, 8 * i:8 * i + 8, :]).then_inc(wgu_in[i], 16)

            for i in range(early // 8):
                load_gu(i)
            sp.wait_ge(ctxc_ready, B)
            sp.wait_ge(wrT_ready, 1)
            sp.wait_ge(sin_done, 1)
            sp.wait_ge(slots_filled, 16)
            sp.wait_ge(acc_filled, 16 * ACCS)
            load_gu(early // 8)
            sp.wait_ge(pv_done, ITEMS)
            sp.wait_ge(qm_ready, ITEMS)
            def load_piece(e):
                sp.dma_start(wgu[:, e:e + CHUNK, :], wgu_src[:, e:e + CHUNK, :]).then_inc(wgu_late, 16)

            sp.wait_ge(scattered, 16 * NSC * (B - 1))
            for e in range(RING, 2 * RING, CHUNK):
                load_piece(e)
            early_part = RING // 2
            sp.wait_ge(wgu_late, ROUND_IN)
            for e in range(2 * RING, 2 * RING + early_part, CHUNK):
                load_piece(e)
            sp.wait_ge(scattered, 16 * NSC * B)

            def load_slots(e, r):
                sp.dma_start(xe[:, r, :], slots[bass.ds(e * C, C), :]).then_inc(xe_in[r], 16)

            for r in range(RING):
                load_slots(r, r)
            for e in range(2 * RING + early_part, 3 * RING, CHUNK):
                load_piece(e)

            def reload(it, r):
                sp.wait_ge(acc_done[r % ACCS], 16 * ((RING // ACCS) * (it - 1) + r // ACCS + 1))
                load_slots(it * RING + r, r)

            sp.wait_ge(wgu_late, 2 * ROUND_IN)
            for r in range(RING):
                if r % CHUNK == 0:
                    load_piece(3 * RING + r)
                reload(1, r)
            with sp.Fori(2, E // RING) as it:
                for r in range(RING):
                    reload(it, r)
            for n, a in enumerate(by_end):
                sp.wait_ge(acc_done[a], 16 * additions(a, E))
                for b in range(B):
                    sp.dma_start(fin[a][:, b * TB:(b + 1) * TB, :],
                                 acc[a].rearrange("(t p) d -> p t d", p=P)[:, b * TB:(b + 1) * TB, :]
                                 ).then_inc(fin_in[n] if n < ACCS - 1 else fin_last_in[b], 16)
            for b in range(B):
                sp.wait_ge(out_ready, b + 1)
                sp.dma_start(of[:, b * TB:(b + 1) * TB, :], xall[:, b * TB:(b + 1) * TB, :]).then_inc(out_done, 16)
            sp.wait_ge(out_done, 16 * B)

        @block.tensor
        def _(pe):
            pe.wait_ge(consts, 1)

            def bank_x(region, b, name):
                need(pe, psx_free, use(region, b, name))

            def do(region, b, name):
                name, _, half = name.partition("_")
                bank_x(region, b, name)
                tiles = (0,) if half else (1,) if region not in ("pro", "tail") else range(TB)
                if name == "xnT":
                    pe.wait_ge(xn_ready, TB * (b + 2))
                    for t in range(TB):
                        for c in range(DC):
                            last = pe.transpose(psX[:, (c * TB + t) * P:(c * TB + t + 1) * P], xn[:, t, c::DC], identf[:])
                elif name == "ctxT":
                    pe.wait_ge(ctxc_ready, b + 2)
                    for t in range(TB):
                        last = pe.transpose(psX[:, t * P:(t + 1) * P], ctxc[:, t, :], identf[:])
                elif name == "q":
                    for t in tiles:
                        for c in range(DC):
                            last = pe.matmul(psX[:, t * D:(t + 1) * D], xT[:, c, t * P:(t + 1) * P],
                                             wq[:, c * D:(c + 1) * D], start=(c == 0), stop=(c == DC - 1))
                elif name in ("kv0", "kv1"):
                    t = int(name[2])
                    last = pe.matmul(psX[:, 0:2 * D], ctxT[:, t * P:(t + 1) * P], wkv[:], start=True, stop=True)
                elif name == "attnT":
                    pe.wait_ge(normed, b * G)
                    for t in range(TB):
                        for c in range(DC):
                            last = pe.transpose(psX[:, (c * TB + t) * P:(c * TB + t + 1) * P], attn[:, t, c::DC], identf[:])
                elif name == "wout":
                    for t in tiles:
                        for c in range(DC):
                            last = pe.matmul(psX[:, t * D:(t + 1) * D], attnT[:, c, t * P:(t + 1) * P],
                                             wout[:, c * D:(c + 1) * D], start=(c == 0), stop=(c == DC - 1))
                elif name == "ynT":
                    pe.wait_ge(y_ready, TB * b)
                    for t in range(TB):
                        for c in range(DC):
                            last = pe.transpose(psX[:, (c * TB + t) * P:(c * TB + t + 1) * P], rows_of(region)[:, t, c:D:DC],
                                                identf[:])
                elif name == "logit":
                    for t in range(TB):
                        for c in range(DC):
                            last = pe.matmul(psX[:, t * E:(t + 1) * E], xT[:, c, t * P:(t + 1) * P], wrT[:, c, :],
                                             start=(c == 0), stop=(c == DC - 1))
                elif name == "rank":
                    pe.wait_ge(chosen_ready, b)
                    need(pe, seen_done, 2 * (b - 1))
                    pe.matmul(psX[:, 0:E], before[:], chosenb[:, 0, :], start=True, stop=False)
                    pe.matmul(psX[:, 0:E], onesb[:], seen[:], start=False, stop=True)
                    pe.matmul(psX[:, E:2 * E], before[:], chosenb[:, 1, :], start=True, stop=False)
                    pe.matmul(psX[:, E:2 * E], onesb[:], chosenb[:, 0, :], start=False, stop=False)
                    last = pe.matmul(psX[:, E:2 * E], onesb[:], seen[:], start=False, stop=True)
                if not half:
                    last.then_inc(psx_full, 1)

            def t1(b, g, par):
                if g == 0:
                    pe.wait_ge(q_split, b + 1)
                    pe.wait_ge(k_split, b + 1)
                need(pe, qk_ready, b * G + g)
                for src, o in ((qsp, 0), (ksp, 2 * N)):
                    for ct in range(2):
                        for t in range(TB):
                            col = par * (TB * H * PARTS) + t * H * PARTS + (4 * g + 2 * ct) * PARTS
                            last = pe.transpose(psT1[:, o + ct * N + t * P:o + ct * N + (t + 1) * P],
                                                src[:, bass.ds(col, P)], identb[:])
                last.then_inc(t1_full, 1)

            def logits(b, g, j):
                t, ct = j % 2, j // 2
                need(pe, max_done, b * H + 4 * g + j - 1)
                pe.matmul(psS[t][:], qT[:, g % 4, ct * N + t * P:ct * N + (t + 1) * P], kT[:, g % 4, ct, :],
                          start=True, stop=True).then_inc(s_full, 1)

            def t2(b, g, par):
                hold(pe, m_ready, b * G + g + 1)
                for ct in range(2):
                    for t in range(TB):
                        col = par * (TB * H * PARTS) + t * H * PARTS + (4 * g + 2 * ct) * PARTS
                        last = pe.transpose(psT2[:, ct * N + t * P:ct * N + (t + 1) * P],
                                            qsp[:, bass.ds(col, P)], identb[:])
                last.then_inc(t2_full, 1)

            def shifted(b, g, j):
                h, ct = j % 2, j // 2
                if j == 0:
                    pe.wait_ge(qm_ready, b * G + g + 1)
                need(pe, exp_done, b * H + 4 * g + j - 1)
                for kc in range(TB):
                    last = pe.matmul(psST[h][:, kc * N:(kc + 1) * N],
                                     kT[:, g % 4, ct, h * N + kc * P:h * N + (kc + 1) * P],
                                     qm[:, g % 2, ct * N:(ct + 1) * N], start=True, stop=True)
                last.then_inc(st_full, 1)

            def pv(b, g):
                pe.wait_ge(exp_done, b * H + 4 * g + 4)
                need(pe, normed, b * G + g)
                if g == 0:
                    pe.wait_ge(v_ready, b + 1)
                for kc in range(TB):
                    for j in range(4):
                        last = pe.matmul(psO[32 * j:32 * j + 32, 0:N],
                                         vaug[:, kc, (4 * g + j) * VCOLS:(4 * g + j + 1) * VCOLS],
                                         probs[:, g % 2, (2 * j + kc) * N:(2 * j + kc + 1) * N],
                                         start=(kc == 0), stop=(kc == TB - 1))
                last.then_inc(pv_done, 1)

            def ot(b, g):
                pe.wait_ge(ot_ready, b * G + g + 1)
                for t in range(TB):
                    last = pe.transpose(ps_ot[:, t * P:(t + 1) * P], otsb[:, g % 2, t * P:(t + 1) * P], identf[:])
                last.then_inc(ot_turned, 1)

            def step(region, b, g):
                one, two, three = (item(region, b, g, back) for back in range(1, LAG + 1))
                new = region != "tail"
                jobs = jobs_at(region, g)
                if new:
                    pe.wait_ge(qk_ready, b * G + g + 1)
                    if g < G - 1:
                        t1(b, g + 1, b % 2)
                    elif region != "last":
                        t1(b + 1, 0, (b + 1) % 2)
                    logits(b, g, 0)
                    logits(b, g, 1)
                if one:
                    if two:
                        pe.wait_ge(qm_ready, two[0] * G + two[1] + 1)
                    t2(*one, one[0] % 2)
                if jobs[0]:
                    do(region, b, jobs[0])
                if new:
                    logits(b, g, 2)
                if two:
                    shifted(*two, 0)
                if new:
                    logits(b, g, 3)
                if two:
                    shifted(*two, 1)
                if jobs[1]:
                    do(region, b, jobs[1])
                if three:
                    pv(*three)
                if two:
                    shifted(*two, 2)
                    shifted(*two, 3)
                if three:
                    ot(*three)
                if jobs[2]:
                    do(region, b, jobs[2])

            do("pro", -1, "ctxT")
            pe.wait_ge(wkv_in, 16)
            do("pro", -1, "kv0")
            do("pro", -1, "kv1")
            do("pro", -1, "xnT")
            pe.wait_ge(wq_in, 16)
            do("pro", -1, "q")
            pe.wait_ge(small_in, 64)
            for c in range(DC):
                last = pe.transpose(psO[:, c * E:(c + 1) * E], rw[:, c::DC], identf[0:E, 0:E])
            last.then_inc(rw_T, 1)
            pe.wait_ge(pads, 2)
            t1(0, 0, 0)
            pe.wait_ge(wrT_ready, 1)
            pe.wait_ge(wout_in, 16)

            def batch(region, b):
                for g in range(G):
                    step(region, b, g)

            regions(pe, batch)
            for g in range(LAG):
                step("tail", B, g)
            for name in epi:
                do("tail", B, name)

            pe.wait_ge(psx_free, BASE_TAIL + len(TAIL))
            for s in (*wd_in, *wgu_in):
                pe.wait_ge(s, 16)

            def to_cols(e, par, r, rounds):
                pe.wait_ge(xe_in[r], 16 * rounds)
                need(pe, xeT_ready, e - 1)
                for c in range(DC):
                    last = pe.transpose(bank_xT[par][:, c * C:(c + 1) * C], xe[:, r, c:D:DC], identf[:])
                last.then_inc(xeT_full, 1)

            def gate_up(e, par):
                pe.wait_ge(xeT_ready, e + 1)
                need(pe, h_ready, e - 1)
                for c in range(DC):
                    last = pe.matmul(bank_gu[par][:, 0:I2], xeT[:, par, c * C:(c + 1) * C],
                                     wgu[:, e, c * I2:(c + 1) * I2], start=(c == 0), stop=(c == DC - 1))
                last.then_inc(gu_full, 1)

            def turn_h(e, par):
                pe.wait_ge(h_ready, e + 1)
                need(pe, hT_ready, e - 1)
                pe.transpose(bank_hT[par][0:I, 0:C], hsb[:, par, :], identf[:]).then_inc(hT_full, 1)

            def down(e, par):
                pe.wait_ge(hT_ready, e + 1)
                need(pe, ye_ready, e - 1)
                pe.matmul(bank_y[par][:, 0:D], hT[0:I, par, :], wd[0:I, e, :], start=True, stop=True).then_inc(y_full, 1)

            def estep(s, k, it=0):
                first, final = isinstance(s, int) and s < 1, isinstance(s, int) and s > E - 3
                if not final:
                    e = s + 2
                    to_cols(e, k % 2, (k + 2) % RING, it + (k + 2) // RING + 1)
                if not (isinstance(s, int) and (s + 1 < 0 or s + 1 >= E)):
                    gate_up(s + 1, (k + 1) % 2)
                if not (isinstance(s, int) and (s < 0 or s >= E)):
                    turn_h(s, k % 2)
                if not first:
                    down(s - 1, (k + 1) % 2)

            LOOPS = (E - 5) // RING
            for s in range(-2, 3):
                estep(s, s)
            with pe.Fori(0, LOOPS) as it:
                pe.wait_ge(wgu_late, ROUND_IN * (it + 1))
                for k in range(3, RING + 3):
                    estep(it * RING + k, k, it)
            for s in range(LOOPS * RING + 3, E + 1):
                estep(s, s)

        @block.scalar
        def _(act):
            def take_ctx(b):
                act.copy(ctxc[:], ctxall[:, bass.ds(b * TB, TB), :]).then_inc(ctxc_ready, 1)

            def do(region, b, name):
                if name in (None, "q_a", "wout_a", "wout", "logit", "rank"):
                    return
                act.wait_ge(psx_full, use(region, b, name) + 1)
                if name in ("xnT", "ynT"):
                    act.copy(xT[:].rearrange("p c n -> p (c n)"), psX[:]).then_inc(psx_free, 1)
                elif name == "ctxT":
                    act.copy(ctxT[:], psX[:, 0:N]).then_inc(psx_free, 1)
                elif name == "q":
                    need(act, q_rot, b + 1)
                    act.copy(qsb[:], psX[:]).then_inc(psx_free, 1)
                elif name in ("kv0", "kv1"):
                    t = int(name[2])
                    need(act, v_ready, b + 1)
                    act.copy(vstage[:, t, :], psX[:, D:2 * D]).then_inc(v_staged, 1)
                    need(act, k_rot, b + 1)
                    act.copy(ksb[:, t * D:(t + 1) * D], psX[:, 0:D]).then_inc(psx_free, 1)
                elif name == "attnT":
                    act.copy(attnT[:].rearrange("p c n -> p (c n)"), psX[:]).then_inc(psx_free, 1)

            def evac_qk(n, slot):
                act.wait_ge(t1_full, n + 1)
                act.copy(qT[:, slot, :], psT1[:, 0:2 * N])
                for h in range(2):
                    last = act.copy(kT[64 * h:64 * h + 64, slot, :, h * N:(h + 1) * N],
                                    psT1[64 * h:64 * h + 64, 2 * N:4 * N].rearrange("p (c n) -> p c n", c=2))
                last.then_inc(qk_ready, 1)

            def expo(b, g, j):
                act.wait_ge(st_full, b * H + 4 * g + j + 1)
                if j == 0:
                    need(act, pv_done, b * G + g - 1)
                act.activation(probs[:, g % 2, j * 2 * N:(j + 1) * 2 * N], psST[j % 2][:], ACT.Exp,
                               scale=SCALE).then_inc(exp_done, 1)

            def evac_qm(b, g):
                act.wait_ge(t2_full, b * G + g + 1)
                act.copy(qm[:, g % 2, :], psT2[:, 0:2 * N]).then_inc(qm_ready, 1)

            def evac_ot(b, g):
                act.wait_ge(pv_done, b * G + g + 1)
                act.copy(otsb[:, g % 2, :], psO[:, 0:N]).then_inc(ot_ready, 1)

            def copy_k(b, part):
                to = parts_of(ksp, b)
                if part == "hi":
                    if not isinstance(b, int) or b > 1:
                        hold(act, t1_full, (b - 1) * G)
                    hold(act, k_rot, b + 1)
                    act.copy(to[:, :, 4:6, :], spread(by_head(ksb), 2))
                    act.copy(to[:, :, 0, :], by_head(ksb)).then_inc(k_hi, 1)
                else:
                    hold(act, k_rest, b + 1)
                    act.copy(to[:, :, 1:4:2, :], spread(by_head(rt), 2)).then_inc(k_mid, 1)

            def copy_v(b):
                act.wait_ge(v_staged, TB * (b + 1))
                act.copy(vaug[:].rearrange("p t (h c) -> p (t h) c", c=VCOLS)[:, :, 0:HD],
                         vstage[:].rearrange("p t (h d) -> p (t h) d", d=HD)).then_inc(v_ready, 1)

            def weights_of(b):
                act.wait_ge(nbest_ready, b)
                need(act, weighed, b - 1)
                for t in range(TB):
                    act.activation(exp8[:, t, :], best[:, t, :], ACT.Exp, bias=nbest[:, t:t + 1],
                                   accum_out=wsum[:, t:t + 1])
                    last = act.activation(expl[:, t, :], logit[:, t, :], ACT.Exp, bias=nbest[:, t:t + 1])
                last.then_inc(expl_ready, 1)

            def step(region, b, g):
                one, two, three = (item(region, b, g, back) for back in range(1, LAG + 1))
                new = region != "tail"
                jobs = jobs_at(region, g)
                if g == 0 and region in ("first", "middle"):
                    take_ctx(b + 1)
                if new and (g < G - 1 or region != "last"):
                    evac_qk(b * G + g + 1, (g + 1) % 4)
                do(region, b, jobs[0])
                if one and qm_by_act(region, g):
                    evac_qm(*one)
                if two:
                    expo(*two, 0)
                    expo(*two, 1)
                do(region, b, jobs[1])
                if three:
                    evac_ot(*three)
                if new and g == 2:
                    copy_v(b)
                if two:
                    expo(*two, 2)
                    expo(*two, 3)
                do(region, b, jobs[2])
                if g == 6 and region in ("middle", "last"):
                    weights_of(b)
                if region in ("first", "middle") and g in K_COPIES:
                    copy_k(b + 1, K_COPIES[g])

            act.wait_ge(ctx_in, 16)
            take_ctx(0)
            for name in ("ctxT", "kv0", "kv1"):
                do("pro", -1, name)
            act.wait_ge(tables, 1)
            c2 = cosT[:].rearrange("p t (f a) -> p t f a", a=2)
            s2 = sinT[:].rearrange("p t (f a) -> p t f a", a=2)
            act.activation(c2[:, :, :, 0], cosr[:], ACT.Sin)
            act.activation(c2[:, :, :, 1], cosr[:], ACT.Sin)
            act.activation(s2[:, :, :, 1], red[:], ACT.Sin)
            act.activation(s2[:, :, :, 0], red[:], ACT.Sin, scale=-1.0).then_inc(sin_done, 1)
            do("pro", -1, "xnT")
            do("pro", -1, "q")
            copy_k(0, "hi")
            copy_k(0, "mid")
            act.wait_ge(small_in, 64)
            act.activation(gates[:, 2:4], gates[:, 0:2], ACT.Tanh).then_inc(gates_ready, 1)
            act.wait_ge(ctx_rest_in, 16)
            evac_qk(0, 0)

            def batch(region, b):
                for g in range(G):
                    step(region, b, g)

            regions(act, batch)
            for g in range(LAG):
                step("tail", B, g)
            do("tail", B, "attnT")
            do("tail", B, "ynT")
            weights_of(B)

            def silu(e, par):
                act.wait_ge(gu_full, e + 1)
                need(act, h_ready, e - 1)
                act.activation(sg[:, par, :], bank_gu[par][:, 0:I], ACT.Silu).then_inc(sg_ready, 1)

            def weigh(e, r, rounds):
                act.wait_ge(y_full, e + 1)
                if isinstance(e, int) and e >= ACCS:
                    act.wait_ge(acc_done[acc_of(e - ACCS)], 16 * additions(acc_of(e - ACCS), e - ACCS + 1))
                else:
                    need(act, acc_done[r % ACCS], 16 * ((RING // ACCS) * rounds + r // ACCS))
                act.activation(ye[:, r % ACCS, :], bank_y[r % 2][:, 0:D], ACT.Copy,
                               scale=xe[:, r, bass.ds(D + e, 1)]).then_inc(ye_ready, 1)

            silu(0, 0)
            silu(1, 1)
            for r in range(RING):
                silu(r + 2, r % 2)
                weigh(r, r, 0)
            with act.Fori(1, E // RING - 1) as it:
                for r in range(RING):
                    silu(it * RING + r + 2, r % 2)
                    weigh(it * RING + r, r, it)
            for r in range(RING):
                e = E - RING + r
                if e + 2 < E:
                    silu(e + 2, r % 2)
                weigh(e, r, E // RING - 1)

        @block.vector
        def _(dve):
            LS = Links(dve, stat_links, 0)

            def statistics(tiles):
                for t in tiles:
                    last = dve.bn_stats(stat1[:, t, :], xall[:, t, :])
                LS.link(last)
                for t in tiles:
                    last = dve.bn_aggr(mv1[:, t, :], stat1[:, t, :])
                last.then_inc(stats1, 1)

            dve.wait_ge(x_in, 16)
            statistics(range(TB))
            LT = Links(dve, table_links, 0)
            dve.wait_ge(pos_in, 16)
            freqs = [10000.0 ** (-f / HALF) for f in range(HALF)]
            a4 = ang[:].rearrange("p t (a f) -> p t a f", f=HALF)
            for f in range(HALF):
                last = dve.tensor_scalar(a4[:, :, :, f], pos[:], freqs[f], None, ALU.mult)
            LT.link(last)
            LT.link(dve.tensor_scalar(turns[:], ang[:], 1.0 / TWO_PI, MAGIC, ALU.mult, ALU.add))
            LT.link(dve.tensor_scalar(turns[:], turns[:], MAGIC, None, ALU.subtract))
            hi, rest1 = two_part(TWO_PI)
            LT.link(dve.scalar_tensor_tensor(red[:], turns[:], -hi, ang[:], ALU.mult, ALU.add))
            LT.link(dve.scalar_tensor_tensor(red[:], turns[:], -rest1, red[:], ALU.mult, ALU.add))
            LT.link(dve.tensor_scalar(cosr[:], red[:], TWO_PI / 4, None, ALU.add))
            LT.link(dve.tensor_scalar(over[:], cosr[:], PI_F, -TWO_PI, ALU.is_gt, ALU.mult))
            LT.link(dve.tensor_tensor(cosr[:], cosr[:], over[:], ALU.add))
            LT.link(dve.tensor_scalar(cosr[:], cosr[:], PI_F, -PI_F, ALU.min, ALU.max))
            dve.tensor_scalar(red[:], red[:], PI_F, -PI_F, ALU.min, ALU.max).then_inc(tables, 1)

            def normalise(b, t):
                dve.tensor_scalar(xn[:, t, :], xall[:, bass.ds(b * TB + t, 1), :].rearrange("p a d -> p (a d)"),
                                  mv1[:, bass.ds(b * TB + t, 1), 0], rstd1[:, bass.ds(b * TB + t, 1)],
                                  ALU.subtract, ALU.mult).then_inc(xn_ready, 1)

            def split_q(b, part):
                to, v, left = parts_of(qsp, b), by_head(qsb), by_head(rest)
                if part == 0:
                    dve.wait_ge(q_rot, b + 1)
                    dve.tensor_copy(to[:, :, PROD // HD, 0:2], zeros[:].unsqueeze(1).to_broadcast([P, TB * H, 2]))
                    dve.tensor_copy(to[:, :, 0:3, :], spread(v, 3)).then_inc(q_split_links, 1)
                    return
                if part == 1:
                    need(dve, q_split, b)
                hold(dve, q_split_links, 3 * b + part)
                if part == 1:
                    dve.tensor_tensor(left, v, to[:, :, 0, :], ALU.subtract).then_inc(q_split_links, 1)
                elif part == 2:
                    dve.tensor_copy(to[:, :, 3:5, :], spread(left, 2)).then_inc(q_split_links, 1)
                else:
                    dve.tensor_tensor(to[:, :, 5, :], left, to[:, :, 3, :], ALU.subtract).then_inc(q_split, 1)

            def row_max(b, g, j):
                dve.wait_ge(s_full, b * H + 4 * g + j + 1)
                if j == 0:
                    need(dve, m_ready, b * G + g - 1)
                t, ct = j % 2, j // 2
                dve.tensor_reduce(nmax[:, g % 2, t, 2 * ct:2 * ct + 2], psS[t][:].rearrange("p (h k) -> p h k", h=2), AX.X, ALU.max,
                                  negate=True).then_inc(max_done, 1)

            def store_max(b, g, part):
                size = TB * H * PARTS
                to = qsp[:, bass.ds((b % 2) * size, size)].rearrange("p (t h r) -> p t h r", t=TB, r=PARTS)
                to = to[:, :, 4 * g:4 * g + 4, :]
                if part == 0:
                    dve.wait_ge(max_done, b * H + 4 * g + 4)
                    dve.tensor_copy(to[:, :, :, PROD], nmax[:, g % 2]).then_inc(mhi_done, 1)
                else:
                    dve.wait_ge(mhi_done, b * G + g + 1)
                    dve.tensor_tensor(to[:, :, :, PROD + 1], nmax[:, g % 2], to[:, :, :, PROD],
                                      ALU.subtract).then_inc(m_ready, 1)

            def norm(b, g):
                o = ps_ot.rearrange("p (t j c) -> p t j c", t=TB, j=4)
                dve.wait_ge(ot_turned, b * G + g + 1)
                dve.reciprocal(rden[:], o[:, :, :, DEN]).then_inc(rden_done, 1)
                dve.wait_ge(rden_done, b * G + g + 1)
                dve.tensor_tensor(attn[:, :, g * 32:(g + 1) * 32].rearrange("p t (j d) -> p t j d", d=HD),
                                  o[:, :, :, 0:HD], rden[:].unsqueeze(3).to_broadcast([P, TB, 4, HD]),
                                  ALU.mult).then_inc(normed, 1)

            def evac_qm(b, g):
                dve.wait_ge(t2_full, b * G + g + 1)
                dve.tensor_copy(qm[:, g % 2, :], psT2[:, 0:2 * N]).then_inc(qm_ready, 1)

            LN_LINKS, ROUTE_LINKS = 2, 6

            def residual(region, b, part):
                n = use(region, b, "wout")
                mine = xall[:, bass.ds((b - 1) * TB, TB), :]
                if part == 0:
                    dve.wait_ge(biased, b)
                    dve.wait_ge(psx_full, n + 1)
                    dve.scalar_tensor_tensor(mine, psX[:].rearrange("p (t d) -> p t d", t=TB), gates[:, 2:3], mine,
                                             ALU.mult, ALU.add).then_inc(psx_free, 1)
                elif part == 1:
                    hold(dve, psx_free, n + 1)
                    for t in range(TB):
                        last = dve.bn_stats(stat2[:, t, :],
                                            xall[:, bass.ds((b - 1) * TB + t, 1), :].rearrange("p a d -> p (a d)"))
                    last.then_inc(ln_links, 1)
                elif part == 2:
                    hold(dve, ln_links, (b - 1) * LN_LINKS + 1)
                    for t in range(TB):
                        last = dve.bn_aggr(mv2[:, t, :], stat2[:, t, :])
                    last.then_inc(ln_links, 1)
                else:
                    dve.wait_ge(ln_links, (b - 1) * LN_LINKS + 2)
                    dve.tensor_scalar(mv2[:, :, 1], mv2[:, :, 1], 1e-5, None, ALU.add).then_inc(stats2, 1)

            def second_norm(region, b, t):
                dve.wait_ge(rstd2_ready, b)
                if region == "tail":
                    dve.wait_ge(psx_full, BASE_LAST)
                else:
                    need(dve, scattered, 16 * NSC * (b - 1))
                dve.tensor_scalar(rows_of(region)[:, t, 0:D], xall[:, bass.ds((b - 1) * TB + t, 1), :].rearrange("p a d -> p (a d)"),
                                  mv2[:, t, 0:1], rstd2[:, t:t + 1], ALU.subtract, ALU.mult).then_inc(y_ready, 1)

            def choose(region, b, part):
                n = use(region, b, "logit")
                links = (b - 1) * ROUTE_LINKS
                if part == 0:
                    dve.wait_ge(psx_full, n + 1)
                    dve.tensor_copy(logit[:].rearrange("p t e -> p (t e)"), psX[:, 0:TB * E]).then_inc(psx_free, 1)
                elif part == 1:
                    hold(dve, psx_free, n + 1)
                    for t in range(TB):
                        last = dve.max(best[:, t, :], logit[:, t, :])
                    last.then_inc(route_links, 1)
                elif part == 2:
                    dve.wait_ge(route_links, links + 1)
                    dve.tensor_scalar(nbest[:], best[:, :, 0], -1.0, None, ALU.mult).then_inc(nbest_ready, 1)
                    for t in range(TB):
                        last = dve.match_replace(cut[:, t, :], best[:, t, :], logit[:, t, :], -3.0e38)
                    last.then_inc(route_links, 1)
                elif part == 3:
                    dve.wait_ge(route_links, links + 2)
                    need(dve, weighed, b - 1)
                    dve.tensor_tensor(chosen[:], cut[:], logit[:], ALU.not_equal).then_inc(route_links, 1)
                else:
                    dve.wait_ge(route_links, links + 3)
                    need(dve, seen_done, 2 * (b - 1))
                    dve.tensor_copy(chosenb[:], chosen[:]).then_inc(chosen_ready, 1)

            def place_choice(region, b, part):
                n = use(region, b, "rank")
                links = (b - 1) * ROUTE_LINKS + 3
                rank = psX[:, 0:TB * E].rearrange("p (t e) -> p t e", t=TB)
                if part == 0:
                    dve.wait_ge(psx_full, n + 1)
                    dve.tensor_scalar(drop[:], rank, float(C), 2.0 * E * C, ALU.is_ge, ALU.mult)
                    dve.tensor_tensor(place[:], rank, slot0[:].rearrange("p (t e) -> p t e", t=TB),
                                      ALU.add).then_inc(route_links, 1)
                elif part == 1:
                    dve.wait_ge(route_links, links + 1)
                    dve.tensor_tensor(place[:], place[:], drop[:], ALU.max).then_inc(psx_free, 1)
                elif part == 2:
                    dve.wait_ge(psx_free, n + 1)
                    dve.scalar_tensor_tensor(place[:], place[:], 1.0, chosen[:], ALU.add, ALU.mult).then_inc(route_links, 1)
                elif part == 3:
                    hold(dve, route_links, links + 2)
                    for t in range(TB):
                        last = dve.max(best8[:, t, :], place[:, t, :])
                    last.then_inc(route_links, 1)
                else:
                    dve.wait_ge(route_links, links + 3)
                    if region == "tail":
                        dve.wait_ge(scattered, 16 * NSC * (B - 1))
                    dve.tensor_scalar(idx[:], best8[:], 1.0, None, ALU.subtract).then_inc(idx_ready, 1)

            def factor(b):
                need(dve, weighed, b - 1)
                dve.wait_ge(expl_ready, b)
                dve.reciprocal(wrec[:], wsum[:]).then_inc(wrec_ready, 1)

            BESIDE = {0: ([], ["n0", "n1"], [], [], []),
                      3: ([], [], [], ["q0"], ["q1"]),
                      4: (["q2"], ["r0"], ["r1"], ["r2"], ["r3"]),
                      5: ([], ["y0"], ["y1"], ["q3"], []),
                      6: (["c0"], ["c1"], ["c2"], ["c3"], ["c4"]),
                      7: ([], ["p0"], ["w0", "p1"], ["p2"], ["p3", "p4"])}
            def beside(region, b, g, where):
                for name in BESIDE.get(g, [[]] * 5)[where]:
                    kind, part = name[0], int(name[1])
                    if region in ("first", "middle"):
                        if kind == "n":
                            normalise(b + 1, part)
                        elif kind == "q":
                            split_q(b + 1, part)
                    if region in ("middle", "last"):
                        if kind == "r":
                            residual(region, b, part)
                        elif kind == "y":
                            second_norm(region, b, part)
                        elif kind == "c":
                            choose(region, b, part)
                        elif kind == "p":
                            place_choice(region, b, part)
                        elif kind == "w":
                            factor(b)

            def step(region, b, g):
                one, three = item(region, b, g, 1), item(region, b, g, LAG)
                new = region != "tail"
                if new:
                    row_max(b, g, 0)
                beside(region, b, g, 0)
                if new:
                    row_max(b, g, 1)
                if one and not qm_by_act(region, g):
                    evac_qm(*one)
                beside(region, b, g, 1)
                if new:
                    row_max(b, g, 2)
                beside(region, b, g, 2)
                if new:
                    row_max(b, g, 3)
                if new:
                    store_max(b, g, 0)
                beside(region, b, g, 3)
                if new:
                    store_max(b, g, 1)
                if g == LAG and region in ("middle", "last"):
                    dve.wait_ge(psx_full, use(region, b, "attnT") + 1)
                if three:
                    norm(*three)
                beside(region, b, g, 4)

            dve.wait_ge(rstd1_ready, 1)
            for t in range(TB):
                normalise(0, t)
            dve.wait_ge(x_rest_in, 16)
            statistics(range(TB, NT))
            dve.wait_ge(sin_done, 1)
            dve.wait_ge(psx_free, use("pro", -1, "q") + 1)
            turn(dve, 0, "q", rest[:], probs[:, 0, 0:TB * D], turn_links, 1)
            dve.wait_ge(pads, 1)
            for part in range(4):
                split_q(0, part)
            dve.wait_ge(rw_T, 1)
            dve.tensor_copy(wrT[:].rearrange("p c e -> p (c e)"), psO[:, 0:DC * E]).then_inc(wrT_ready, 1)
            dve.wait_ge(rstd1_ready, 2)

            def batch(region, b):
                for g in range(G):
                    step(region, b, g)

            regions(dve, batch)
            for g in range(LAG):
                step("tail", B, g)
            for part in range(4):
                residual("tail", B, part)
            for t in range(TB):
                second_norm("tail", B, t)
            for part in range(5):
                choose("tail", B, part)
            factor(B)
            for part in range(5):
                place_choice("tail", B, part)

            def evac_xT(e, par):
                dve.wait_ge(xeT_full, e + 1)
                need(dve, gu_full, e - 1)
                dve.tensor_copy(xeT[:, par, :], bank_xT[par][:, 0:DC * C]).then_inc(xeT_ready, 1)

            def times_up(e, par):
                dve.wait_ge(sg_ready, e + 1)
                need(dve, hT_full, e - 1)
                dve.tensor_tensor(hsb[:, par, :], bank_gu[par][:, I:I2], sg[:, par, :], ALU.mult).then_inc(h_ready, 1)

            def evac_hT(e, par):
                dve.wait_ge(hT_full, e + 1)
                need(dve, y_full, e - 1)
                dve.tensor_copy(hT[0:I, par, :], bank_hT[par][0:I, 0:C]).then_inc(hT_ready, 1)

            def estep(s, k):
                known = isinstance(s, int)
                if not (known and s + 2 >= E):
                    evac_xT(s + 2, k % 2)
                if not (known and (s + 1 < 0 or s + 1 >= E)):
                    times_up(s + 1, (k + 1) % 2)
                if not (known and (s < 0 or s >= E)):
                    evac_hT(s, k % 2)

            for s in range(-2, 3):
                estep(s, s)
            LOOPS = (E - 5) // RING
            with dve.Fori(0, LOOPS) as it:
                for k in range(3, RING + 3):
                    estep(it * RING + k, k)
            for s in range(LOOPS * RING + 3, E + 1):
                estep(s, s)

            for n, a in enumerate(by_end[:-1]):
                dve.wait_ge(fin_in[n], 16 * B)
                need(dve, fin_links, n)
                dve.scalar_tensor_tensor(xall[:], fin[a][:], gates[:, 3:4], xall[:], ALU.mult,
                                         ALU.add).then_inc(fin_links, 1)
            for b in range(B):
                mine = xall[:, b * TB:(b + 1) * TB, :]
                dve.wait_ge(fin_last_in[b], 16)
                dve.wait_ge(fin_links, ACCS - 1)
                dve.scalar_tensor_tensor(mine, fin[by_end[-1]][:, b * TB:(b + 1) * TB, :], gates[:, 3:4], mine,
                                         ALU.mult, ALU.add).then_inc(out_ready, 1)

        @block.gpsimd
        def _(pool):
            LP = Links(pool, pool_links, 0)
            LP.link(pool.memset(zrow[:], 0.0))
            pool.iota(zrow[:, ID:ID + 1].bitcast(I32), [[0, 1]], base=T, channel_multiplier=1).then_inc(zrow_ready, 1)
            pool.memset(before[:], 0.0)
            LP.link(pool.memset(identf[:], 0.0))
            LP.link(pool.affine_select(out=identf[:], in_=identf[:], compare_op=ALU.not_equal, fill=1.0, base=0,
                                       pattern=[[-1, P]], channel_multiplier=1))
            pool.tensor_copy(identb[:], identf[:]).then_inc(consts, 1)
            pool.memset(half_neg[:], -0.5)
            pool.memset(zeros[:], 0.0)
            q16 = qsp[:].rearrange("p (n r) -> p n r", r=PARTS)
            k16 = ksp[:].rearrange("p (n r) -> p n r", r=PARTS)
            LP.link(pool.memset(q16[:, :, PROD:PARTS].bitcast(F32), 0.0))

            def rest_of_k(b, part):
                to = parts_of(ksp, b)
                if part == "hi":
                    hold(pool, k_hi, b + 1)
                    pool.tensor_tensor(by_head(rt), by_head(ksb), to[:, :, 0, :], ALU.subtract).then_inc(k_rest, 1)
                else:
                    hold(pool, k_mid, b + 1)
                    pool.tensor_tensor(to[:, :, 2, :], by_head(rt), to[:, :, 3, :], ALU.subtract).then_inc(k_split, 1)

            def root1(tiles, n):
                pool.wait_ge(stats1, n)
                LP.link(pool.tensor_scalar(rstd1[:, tiles], mv1[:, tiles, 1], 1e-5, None, ALU.add))
                pool.tensor_tensor(rstd1[:, tiles], rstd1[:, tiles], half_neg[:, tiles], ALU.pow).then_inc(rstd1_ready, 1)

            root1(slice(0, TB), 1)
            pool.memset(k16[:, :, MAXROWS:PARTS].bitcast(F32), 0.0)
            pool.memset(k16[:, :, PROD:MAXROWS], 1.0)
            pool.memset(kT[:].bitcast(F32), 0.0).then_inc(pads, 1)
            pool.wait_ge(sin_done, 1)
            pool.wait_ge(psx_free, use("pro", -1, "kv1") + 1)
            turn(pool, 0, "k", rt[:], rt2[:], rope_links, 1)
            LP.link(pool.memset(vaug[:], 0.0))
            pool.memset(vaug[:].rearrange("p t (h c) -> p (t h) c", c=VCOLS)[:, :, DEN:DEN + 1], 1.0).then_inc(pads, 1)
            rest_of_k(0, "hi")
            rest_of_k(0, "mid")
            root1(slice(TB, NT), 2)
            pool.affine_select(out=before[:], in_=before[:], compare_op=ALU.is_ge, fill=1.0, base=0,
                               pattern=[[-1, P]], channel_multiplier=1)
            pool.memset(onesb[:], 1.0)
            LP.link(pool.memset(seen[:], 0.0))
            pool.iota(ids[:], [[P, NT]], base=0, channel_multiplier=1)
            LP.link(pool.iota(slot_i[:], [[0, TB], [C, E]], base=0, channel_multiplier=0))
            pool.tensor_copy(slot0[:], slot_i[:])
            pool.memset(rows[:, :, ID:ROW], 0.0).then_inc(rows_ready, 1)

            def rotate(region, b, what):
                if what == "k":
                    pool.wait_ge(q_rot, b + 2)
                else:
                    need(pool, k_split, b + 1)
                hold(pool, psx_free, use(region, b, "q" if what == "q" else "kv1") + 1)
                turn(pool, b + 1, what, rt[:], rt2[:], rope_links, 2 * b + (2 if what == "q" else 3))

            def root(b):
                pool.wait_ge(stats2, b)
                pool.tensor_tensor(rstd2[:], mv2[:, :, 1], half_neg[:, 0:TB], ALU.pow).then_inc(rstd2_ready, 1)

            ROOT_FIRST = 3

            def scatter(region, b):
                there = rows_of(region)
                count = b + (region == "tail")
                if region != "tail":
                    need(pool, scattered, 16 * NSC * (b - 1))
                hold(pool, rows_ready, count)
                pool.tensor_copy(there[:, :, ID].bitcast(I32), ids[:, bass.ds((b - 1) * TB, TB)]).then_inc(rows_ready, 1)
                pool.wait_ge(chosen_ready, b)
                pool.wait_ge(expl_ready, b)
                pool.tensor_tensor(wbuf[:], expl[:], chosen[:], ALU.mult).then_inc(weigh_links, 1)
                pool.wait_ge(wrec_ready, b)
                hold(pool, weigh_links, b)
                pool.tensor_tensor(there[:, :, D:ID], wbuf[:], wrec[:].unsqueeze(2).to_broadcast([P, TB, E]),
                                   ALU.mult).then_inc(weighed, 1)
                hold(pool, psx_full, use(region, b, "rank") + 1)
                pool.tensor_tensor(seen[:], seen[:], chosenb[:, 0, :], ALU.add).then_inc(seen_done, 1)
                hold(pool, seen_done, 2 * b - 1)
                pool.tensor_tensor(seen[:], seen[:], chosenb[:, 1, :], ALU.add).then_inc(seen_done, 1)
                pool.wait_ge(weighed, b)
                pool.wait_ge(rows_ready, count + 1)
                hold(pool, idx_ready, b)
                for t in range(TB):
                    for k in range(TOPK):
                        if region == "last" and t * TOPK + k == NSC - ROOT_FIRST:
                            root(B)
                        pool.indirect_dma_start(out=slots, out_offset=bass.IndirectOffsetOnAxis(ap=idx[:, t, k:k + 1], axis=0),
                                                in_=there[:, t, :], in_offset=None, bounds_check=E * C - 1,
                                                oob_is_err=False).then_inc(scattered, 16)

            def bias(b):
                hold(pool, xn_ready, TB * (b + 1))
                mine = xall[:, bass.ds(b * TB, TB), :]
                pool.tensor_tensor(mine, mine, boutg[:].unsqueeze(1).to_broadcast([P, TB, D]), ALU.add).then_inc(biased, 1)

            pool.wait_ge(gates_ready, 1)
            LP.link(pool.tensor_scalar(boutg[:], boutg[:], gates[:, 2:3], None, ALU.mult))
            bias(0)

            def batch(region, b):
                if region != "last":
                    rotate(region, b, "q")
                    rotate(region, b, "k")
                    bias(b + 1)
                if region != "first":
                    root(b)
                if region != "last":
                    rest_of_k(b + 1, "hi")
                    rest_of_k(b + 1, "mid")
                if region != "first":
                    scatter(region, b)
                else:
                    pool.wait_ge(slots_filled, 16)

            regions(pool, batch)
            pool.wait_ge(psx_full, BASE_LAST)
            pool.memset(rows_last[:, :, ID:ROW], 0.0).then_inc(rows_ready, 1)
            scatter("tail", B)

            def add_rows(e, r, rounds):
                a = acc_of(e) if isinstance(e, int) else r % ACCS
                pool.wait_ge(ye_ready, e + 1)
                hold(pool, acc_done[a], 16 * (additions(a, e) if isinstance(e, int) else
                                              (RING // ACCS) * rounds + r // ACCS))
                pool.indirect_dma_start(out=acc[a],
                                        out_offset=bass.IndirectOffsetOnAxis(ap=xe[:, r, ID:ID + 1].bitcast(U32), axis=0),
                                        in_=ye[:, r % ACCS, :], in_offset=None, bounds_check=T + P - 1, oob_is_err=True,
                                        compute_op=ALU.add).then_inc(acc_done[a], 16)

            pool.wait_ge(acc_filled, 16 * ACCS)
            with pool.Fori(0, E // RING - 1) as it:
                for r in range(RING):
                    add_rows(it * RING + r, r, it)
            for r in range(RING):
                add_rows(E - RING + r, r, E // RING - 1)


_INS = ["x", "ctx_1024", "fside_BxSx2_0", "g_xattn", "g_ffn", "L0_xattn_Wq", "L0_xattn_Wkv", "L0_xattn_Wout",
        "L0_xattn_bout", "L0_ffn_router_weight", "L0_ffn_gate_up_proj", "L0_ffn_down_proj"]


def kernel(**inputs):
    import numpy as _np
    import concourse.bacc as _bacc
    from concourse import mybir as _mybir
    from concourse.bass_utils import run_bass_kernel_spmd as _run

    nc = _bacc.Bacc("TRN2", target_bir_lowering=False, num_devices=1)
    arrays, args = {}, []
    for name in _INS:
        a = _np.ascontiguousarray(inputs[name])
        arrays[f"in_{name}"] = a
        args.append(nc.dram_tensor(f"in_{name}", a.shape, _mybir.dt.from_np(a.dtype), kind="ExternalInput").ap())
    shape = inputs["x"].shape
    out = nc.dram_tensor("out_0", shape, _mybir.dt.float32, kind="ExternalOutput").ap()
    flamingo(nc, *args, out)
    r = _run(nc, [arrays], core_ids=[0])
    return r.results[0]["out_0"]
```
